# Optimizing a Trainium2 kernel written in Bass

```python
import numpy as np
import jax
import jax.numpy as jnp

def _softmax(x, axis=-1):
    return jax.nn.softmax(x, axis=axis)

def _gelu(x):
    return jax.nn.gelu(x, approximate=True)

def _silu(x):
    return jax.nn.silu(x)

def _sigmoid(x):
    return jax.nn.sigmoid(x)

def _layernorm(x, axis=-1, eps=1e-05):
    m = jnp.mean(x, axis=axis, keepdims=True)
    v = jnp.var(x, axis=axis, keepdims=True)
    return (x - m) / jnp.sqrt(v + eps)

def _scatter_add(tgt, idx, src, axis=0):
    return tgt.at[idx].add(src)

def _segment_sum(src, seg, n):
    return jax.ops.segment_sum(src, seg, n)
kernel_name = 'mk_conv_seq_d2_conv_nchw192_r2_2932e1'

def setup_inputs(seed: int=0):
    np.random.seed(seed)
    _w = jnp.asarray

    def _rec_inputs():
        import jax
        import jax.numpy as jnp
        _gk = jax.random.key(seed)
        x = -0.0002221 + 1 * jax.random.normal(jax.random.fold_in(_gk, 1), (8, 96, 64, 64), jnp.float32)
        return x
    x = _rec_inputs()

    def _L0_conv_setup():
        import jax, jax.numpy as jnp
        import numpy as np
        B, C, H, W = (8, 96, 64, 64)
        E, HID, TOP_K = (4, 192, 2)
        key = jax.random.key(seed)
        ks = jax.random.split(key, 5)
        sn = lambda k, sh, sc: jax.random.normal(k, sh, jnp.float32) * sc
        return {'x': jax.random.normal(ks[0], (B, C, H, W), jnp.float32), 'router_w': sn(ks[1], (E, C), C ** (-0.5)), 'router_b': jnp.zeros((E,), jnp.float32), 'fc1_w': sn(ks[2], (E, HID, C), C ** (-0.5)), 'fc1_b': jnp.zeros((E, HID), jnp.float32), 'fc2_w': sn(ks[3], (E, C, HID), HID ** (-0.5)), 'fc2_b': jnp.zeros((E, C), jnp.float32), 'scale': jnp.array([0.1], jnp.float32)}
    _L0_conv_all = _L0_conv_setup()
    _L0_conv_in = {k: v for k, v in _L0_conv_all.items() if k in ('router_w', 'router_b', 'fc1_w', 'fc1_b', 'fc2_w', 'fc2_b', 'scale')}
    del _L0_conv_all

    def _L1_conv_setup():
        import jax, jax.numpy as jnp
        import numpy as np
        D_MODEL = 96
        D_STATE = 16
        D_CONV = 4
        EXPAND = 2
        D_INNER = EXPAND * D_MODEL
        DT_RANK = (D_MODEL + 15) // 16
        B_SZ, H_IMG, W_IMG = (4, 32, 32)
        LN_EPS = 1e-05

        def _mamba(x, W_in, conv_w, conv_b, W_xproj, W_dt, b_dt, A_log, D, W_out):
            Bb, L, _ = x.shape
            xz = x @ W_in
            xr, z = jnp.split(xz, 2, axis=-1)
            xc = jnp.transpose(xr, (0, 2, 1))
            xc = jax.lax.conv_general_dilated(xc, conv_w[:, None, :], (1,), [(D_CONV - 1, 0)], dimension_numbers=('NCH', 'OIH', 'NCH'), feature_group_count=D_INNER)
            xr = jax.nn.silu(jnp.transpose(xc + conv_b[None, :, None], (0, 2, 1)))
            dbl = xr @ W_xproj
            dt = jax.nn.softplus(dbl[..., :DT_RANK] @ W_dt + b_dt)
            Bm = dbl[..., DT_RANK:DT_RANK + D_STATE]
            Cm = dbl[..., DT_RANK + D_STATE:]
            A = -jnp.exp(A_log)

            def step(h, inp):
                dt_t, B_t, C_t, x_t = inp
                h = jnp.exp(dt_t[:, :, None] * A) * h + (dt_t * x_t)[:, :, None] * B_t[:, None, :]
                y_t = jnp.einsum('ben,bn->be', h, C_t)
                return (h, y_t)
            h0 = jnp.zeros((Bb, D_INNER, D_STATE), x.dtype)
            xs = (dt.transpose(1, 0, 2), Bm.transpose(1, 0, 2), Cm.transpose(1, 0, 2), xr.transpose(1, 0, 2))
            _, ys = jax.lax.scan(step, h0, xs)
            y = ys.transpose(1, 0, 2) + xr * D
            y = y * jax.nn.silu(z)
            return y @ W_out
        key = jax.random.key(seed)
        ks = jax.random.split(key, 8)
        s = lambda k, shape, sc: jax.random.normal(k, shape, jnp.float32) * sc
        dt_bias = float(np.log(np.expm1(0.01)))
        return {'x': jax.random.normal(ks[0], (B_SZ, D_MODEL, H_IMG, W_IMG), jnp.float32), 'gamma': jnp.ones((D_MODEL,), jnp.float32), 'beta': jnp.zeros((D_MODEL,), jnp.float32), 'W_in': s(ks[1], (D_MODEL, 2 * D_INNER), 0.05), 'conv_w': s(ks[2], (D_INNER, D_CONV), 0.3), 'conv_b': jnp.zeros((D_INNER,), jnp.float32), 'W_xproj': s(ks[3], (D_INNER, DT_RANK + 2 * D_STATE), 0.05), 'W_dt': s(ks[4], (DT_RANK, D_INNER), 0.1), 'b_dt': jnp.full((D_INNER,), dt_bias, jnp.float32), 'A_log': jnp.log(jnp.tile(jnp.arange(1, D_STATE + 1, dtype=jnp.float32), (D_INNER, 1))), 'D': jnp.ones((D_INNER,), jnp.float32), 'W_out': s(ks[5], (D_INNER, D_MODEL), 0.05)}
    _L1_conv_all = _L1_conv_setup()
    _L1_conv_in = {k: v for k, v in _L1_conv_all.items() if k in ('gamma', 'beta', 'W_in', 'conv_w', 'conv_b', 'W_xproj', 'W_dt', 'b_dt', 'A_log', 'D', 'W_out')}
    del _L1_conv_all
    return {'x': x, 'L0_conv_router_w': _L0_conv_in['router_w'], 'L0_conv_router_b': _L0_conv_in['router_b'], 'L0_conv_fc1_w': _L0_conv_in['fc1_w'], 'L0_conv_fc1_b': _L0_conv_in['fc1_b'], 'L0_conv_fc2_w': _L0_conv_in['fc2_w'], 'L0_conv_fc2_b': _L0_conv_in['fc2_b'], 'L0_conv_scale': _L0_conv_in['scale'], 'L1_conv_gamma': _L1_conv_in['gamma'], 'L1_conv_beta': _L1_conv_in['beta'], 'L1_conv_W_in': _L1_conv_in['W_in'], 'L1_conv_conv_w': _L1_conv_in['conv_w'], 'L1_conv_conv_b': _L1_conv_in['conv_b'], 'L1_conv_W_xproj': _L1_conv_in['W_xproj'], 'L1_conv_W_dt': _L1_conv_in['W_dt'], 'L1_conv_b_dt': _L1_conv_in['b_dt'], 'L1_conv_A_log': _L1_conv_in['A_log'], 'L1_conv_D': _L1_conv_in['D'], 'L1_conv_W_out': _L1_conv_in['W_out']}

def reference(x, L0_conv_router_w, L0_conv_router_b, L0_conv_fc1_w, L0_conv_fc1_b, L0_conv_fc2_w, L0_conv_fc2_b, L0_conv_scale, L1_conv_gamma, L1_conv_beta, L1_conv_W_in, L1_conv_conv_w, L1_conv_conv_b, L1_conv_W_xproj, L1_conv_W_dt, L1_conv_b_dt, L1_conv_A_log, L1_conv_D, L1_conv_W_out):
    import jax
    import jax.numpy as jnp

    def _L0_conv_ref(x, router_w, router_b, fc1_w, fc1_b, fc2_w, fc2_b, scale):
        import jax, jax.numpy as jnp
        import numpy as np
        B, C, H, W = (8, 96, 64, 64)
        E, HID, TOP_K = (4, 192, 2)
        b, c, h, w = x.shape
        e = router_w.shape[0]
        tokens = jnp.transpose(x, (0, 2, 3, 1)).reshape(b, h * w, c)
        logits = tokens @ router_w.T + router_b
        topv, topi = jax.lax.top_k(logits, TOP_K)
        wts = jax.nn.softmax(topv, axis=-1)
        gates = jnp.sum(jax.nn.one_hot(topi, e, dtype=tokens.dtype) * wts[..., None], axis=-2)
        out = jnp.zeros_like(tokens)
        for ei in range(e):
            hid = jax.nn.gelu(tokens @ fc1_w[ei].T + fc1_b[ei], approximate=False)
            y_e = hid @ fc2_w[ei].T + fc2_b[ei]
            out = out + gates[..., ei:ei + 1] * y_e
        out = jnp.transpose(out.reshape(b, h, w, c), (0, 3, 1, 2))
        return x + scale[0] * out

    def _L1_conv_ref(x, gamma, beta, W_in, conv_w, conv_b, W_xproj, W_dt, b_dt, A_log, D, W_out):
        import jax, jax.numpy as jnp
        import numpy as np
        D_MODEL = 96
        D_STATE = 16
        D_CONV = 4
        EXPAND = 2
        D_INNER = EXPAND * D_MODEL
        DT_RANK = (D_MODEL + 15) // 16
        B_SZ, H_IMG, W_IMG = (4, 32, 32)
        LN_EPS = 1e-05

        def _mamba(x, W_in, conv_w, conv_b, W_xproj, W_dt, b_dt, A_log, D, W_out):
            Bb, L, _ = x.shape
            xz = x @ W_in
            xr, z = jnp.split(xz, 2, axis=-1)
            xc = jnp.transpose(xr, (0, 2, 1))
            xc = jax.lax.conv_general_dilated(xc, conv_w[:, None, :], (1,), [(D_CONV - 1, 0)], dimension_numbers=('NCH', 'OIH', 'NCH'), feature_group_count=D_INNER)
            xr = jax.nn.silu(jnp.transpose(xc + conv_b[None, :, None], (0, 2, 1)))
            dbl = xr @ W_xproj
            dt = jax.nn.softplus(dbl[..., :DT_RANK] @ W_dt + b_dt)
            Bm = dbl[..., DT_RANK:DT_RANK + D_STATE]
            Cm = dbl[..., DT_RANK + D_STATE:]
            A = -jnp.exp(A_log)

            def step(h, inp):
                dt_t, B_t, C_t, x_t = inp
                h = jnp.exp(dt_t[:, :, None] * A) * h + (dt_t * x_t)[:, :, None] * B_t[:, None, :]
                y_t = jnp.einsum('ben,bn->be', h, C_t)
                return (h, y_t)
            h0 = jnp.zeros((Bb, D_INNER, D_STATE), x.dtype)
            xs = (dt.transpose(1, 0, 2), Bm.transpose(1, 0, 2), Cm.transpose(1, 0, 2), xr.transpose(1, 0, 2))
            _, ys = jax.lax.scan(step, h0, xs)
            y = ys.transpose(1, 0, 2) + xr * D
            y = y * jax.nn.silu(z)
            return y @ W_out
        Bb, C, Hh, Ww = x.shape
        x_flat = x.reshape(Bb, C, Hh * Ww).transpose(0, 2, 1)
        mu = x_flat.mean(-1, keepdims=True)
        var = ((x_flat - mu) ** 2).mean(-1, keepdims=True)
        x_norm = (x_flat - mu) * jax.lax.rsqrt(var + LN_EPS) * gamma + beta
        x_in = jnp.concatenate([x_norm, x_norm[:, ::-1]], axis=0)
        out2 = _mamba(x_in, W_in, conv_w, conv_b, W_xproj, W_dt, b_dt, A_log, D, W_out)
        out_fwd, out_rev = (out2[:Bb], out2[Bb:, ::-1])
        out = (out_fwd + out_rev) * 0.5 + x_flat
        return out.transpose(0, 2, 1).reshape(Bb, C, Hh, Ww)

    def _gn(v, G=32, eps=1e-05):
        B_, C_, H_, W_ = v.shape
        g = v.reshape(B_, G, C_ // G, H_, W_)
        m = jnp.mean(g, axis=(2, 3, 4), keepdims=True)
        s = jnp.var(g, axis=(2, 3, 4), keepdims=True)
        return ((g - m) / jnp.sqrt(s + eps)).reshape(v.shape)

    def _ln_c(v, eps=1e-06):
        m = jnp.mean(v, axis=1, keepdims=True)
        s = jnp.var(v, axis=1, keepdims=True)
        return (v - m) / jnp.sqrt(s + eps)

    def _ln_t(v, eps=1e-05):
        m = jnp.mean(v, axis=-1, keepdims=True)
        s = jnp.var(v, axis=-1, keepdims=True)
        return (v - m) / jnp.sqrt(s + eps)

    def _to_tokens(v):
        B_, C_, H_, W_ = v.shape
        return v.reshape(B_, C_, H_ * W_).transpose(0, 2, 1)

    def _from_tokens(t, like):
        B_, C_, H_, W_ = like.shape
        return t.transpose(0, 2, 1).reshape(B_, C_, H_, W_)
    x = _L0_conv_ref(x, L0_conv_router_w, L0_conv_router_b, L0_conv_fc1_w, L0_conv_fc1_b, L0_conv_fc2_w, L0_conv_fc2_b, L0_conv_scale)
    x = _L1_conv_ref(x, L1_conv_gamma, L1_conv_beta, L1_conv_W_in, L1_conv_conv_w, L1_conv_conv_b, L1_conv_W_xproj, L1_conv_W_dt, L1_conv_b_dt, L1_conv_A_log, L1_conv_D, L1_conv_W_out)
    return x

_drawn_inputs = setup_inputs


def setup_inputs(seed=0):
    import zlib

    import numpy as np

    out = dict(_drawn_inputs(seed))
    spreads = {'L0_conv_router_b': (0.0, 0.8),
     'L0_conv_fc1_b': (0.0, 0.8),
     'L0_conv_fc2_b': (0.0, 0.8),
     'L1_conv_gamma': (1.0, 0.6),
     'L1_conv_beta': (0.0, 0.8),
     'L1_conv_conv_b': (0.0, 0.783),
     'L1_conv_b_dt': (-4.600165843963623, 0.6),
     'L1_conv_D': (1.0, 0.6)}
    factors = {'L1_conv_W_xproj': 8.0, 'L1_conv_W_dt': 8.0, 'L1_conv_A_log': 8.0}
    for name, (base, spread) in spreads.items():
        noise = np.random.default_rng([zlib.crc32(name.encode()), seed]).standard_normal(out[name].shape)
        drawn = base * np.exp(spread * noise) if base else spread * noise
        out[name] = jnp.asarray(drawn.astype(out[name].dtype))
    for name, factor in factors.items():
        out[name] = (out[name] * factor).astype(out[name].dtype)
    return out
```

```python
import concourse.bass as bass
from concourse import mybir
from contextlib import ExitStack
import numpy as np

IMGS, C, PIX = 8, 96, 4096
E, HID = 4, 192
DI, NST, RANK, TAPS = 192, 16, 6, 4
P = 128
CH = 512
NCH = PIX // CH
NT = DI * NST // P
CPT = P // NST
HT = E * HID // P
GRP = 32
NG = DI // GRP
DR = DI - P
BLK = IMGS * PIX // P
WIN = CH + 2 * (TAPS - 1)
PADW = PIX + 2 * (TAPS - 1)
BODIES = 2 * NCH
LN_EPS = 1e-5
SP_MAX = 40.0
BATCH = 4
NB = NT // BATCH
LEAD_DT, LEAD_DTX = 4, 2

TILES = [(GRP * j + CPT * r, r, j) for r in range(4) for j in range(4)]
TILES += [(P + GRP * j + CPT * r, r, j) for r in range(4) for j in range(2)]
NT0 = P // CPT


def selectors():
    sel = np.zeros((3 * GRP, 4, P), np.float32)
    red = np.zeros((P, 4, GRP), np.float32)
    for p in range(P):
        for r in range(4):
            sel[CPT * r + p // NST::GRP, r, p] = 1
            red[p, r, CPT * r + p // NST] = 1
    gate = np.zeros((3 * E, HT, P), np.float32)
    for m in range(HT):
        for p in range(P):
            gate[(m * P + p) // HID::E, m, p] = 1
    return {
        "c_sel": sel.reshape(3 * GRP, -1), "c_red": red.reshape(P, -1), "c_gate": gate.reshape(3 * E, -1),
        "c_ident": np.eye(P, dtype=np.float32), "c_mean": np.full((C, C), 1.0 / C, np.float32),
    }


def bank_uses(odd, next_rev, fin, moe=True, prep=True):
    uses = []
    if prep:
        uses += [("U0", 0), ("U1", 1)]
        if next_rev:
            uses += [("Z0", 0), ("Z1", 1)]
        uses += [("D0", 0), ("D1", 1), ("B", 0), ("C", 1)]
    if fin:
        uses += [("OUT", 1)]
    if moe and not odd:
        uses += [("GT", 1)]
        uses += [(f"H{m}", m % 2) for m in range(HT)]
        uses += [(f"G{m}", m % 2) for m in range(HT)]
    if moe and odd:
        uses += [("Y2", 0), ("MU", 1), ("VAR", 0)]
    return uses


def count(uses, bank):
    return sum(b == bank for _, b in uses)


class Uses:

    def __init__(self, uses, base):
        self.at, seen = {}, [0, 0]
        for name, bank in uses:
            self.at[name] = (bank, base[bank] + seen[bank])
            seen[bank] += 1


PRO_PIECE = bank_uses(False, False, False, prep=False) + bank_uses(True, False, False, prep=False)
PRO_PREP = bank_uses(False, False, False, moe=False)
PRO = [count(PRO_PIECE, i) * NCH + count(PRO_PREP, i) for i in (0, 1)]


def kinds():
    half = NCH // 2
    return [(0, 0, half - 1, False, False), (0, half - 1, 1, True, False),
            (1, 0, 1, False, False), (1, 1, half - 2, False, True), (1, half - 1, 1, True, True)]


def pair_uses(run):
    rev, _, _, last, fin = run
    return (bank_uses(False, rev == 1, fin), bank_uses(True, (rev == 1) != last, rev == 1))


TAIL = [("OUT", 1)]
PER_IMAGE = [sum(n * (count(a, i) + count(b, i)) for run in kinds() for n in [run[2]] for a, b in [pair_uses(run)])
             + count(TAIL, i) for i in (0, 1)]


def bodies(eng, body, tail):
    with eng.Fori(0, IMGS) as img:
        start = [PRO[i] + img * PER_IMAGE[i] for i in (0, 1)]
        for run in kinds():
            rev, p0, pairs, last, fin = run
            even, odd = pair_uses(run)
            per = [count(even, i) + count(odd, i) for i in (0, 1)]

            def pair(q):
                base = [start[i] + (q - p0) * per[i] for i in (0, 1)]
                body(img, q, rev, 0, last, fin, Uses(even, base))
                base = [base[i] + count(even, i) for i in (0, 1)]
                body(img, q, rev, 1, last, rev == 1, Uses(odd, base))

            if pairs > 1:
                with eng.Fori(p0, p0 + pairs) as q:
                    pair(q)
            else:
                pair(p0)
            start = [start[i] + pairs * per[i] for i in (0, 1)]
        tail(img, Uses(TAIL, start))


def chunk_of(q, rev, odd):
    return (NCH - 1 - odd) - q * 2 if rev else q * 2 + odd


def moe_mamba(nc, A):
    f32, bf16 = mybir.dt.float32, mybir.dt.bfloat16
    ALU, ACT, AX = mybir.AluOpType, mybir.ActivationFunctionType, mybir.AxisListType
    ctx = ExitStack()
    with ctx:
        def sb(name, shape, dt=f32):
            return ctx.enter_context(nc.sbuf_tensor(name, shape, dt))

        def sem(name):
            return ctx.enter_context(nc.semaphore(name))

        xn_d = nc.dram_tensor("xn_d", [IMGS, C + 1, PADW], f32, kind="Internal").ap()
        x2_d = nc.dram_tensor("x2_d", [IMGS, C, PIX], f32, kind="Internal").ap()

        w1 = sb("w1", [C, E * HID])
        w2 = sb("w2", [P, HT, C])
        b1 = sb("b1", [P, HT])
        b2f = sb("b2f", [3 * E, C])
        b2r = sb("b2r", [3 * E, C])
        b2s = sb("b2s", [3 * E, 3, C], bf16)
        scl = sb("scl", [P, 1])
        wr = sb("wr", [C, E])
        rb = sb("rb", [P, E])
        w_in = sb("w_in", [C, 2 * DI])
        w_g = sb("w_g", [C + 1, 2 * DI])
        gam = sb("gam", [C, 1])
        bet = sb("bet", [C, 1])
        w_u = sb("w_u", [C + 1, TAPS, DI])
        cb = [sb("cb0", [P, 1]), sb("cb1", [DR, 1])]
        wx = [sb("wx0", [P, RANK + 2 * NST]), sb("wx1", [DR, RANK + 2 * NST])]
        wxT = sb("wxT", [RANK, DI])
        wdt = sb("wdt", [RANK, DI])
        w_d = [sb("wd0", [P, DI]), sb("wd1", [DR, DI])]
        w_b = [sb("wb0", [P, P]), sb("wb1", [DR, P])]
        w_c = [sb("wc0", [P, P]), sb("wc1", [DR, P])]
        bd = [sb("bd0", [P, 1]), sb("bd1", [DR, 1])]
        nbd = [sb("nbd0", [P, 1]), sb("nbd1", [DR, 1])]
        amat = sb("amat", [P, NT])
        dvec = [sb("dv0", [P, 1]), sb("dv1", [DR, 1])]
        diag = [sb("dg0", [P, P]), sb("dg1", [DR, P])]
        wo0 = sb("wo0", [P, C])
        wo1 = sb("wo1", [P, C])
        sel = sb("sel", [3 * GRP, 4, P], bf16)
        red = sb("red", [P, 4, GRP])
        gsel = sb("gsel", [3 * E, HT, P], bf16)
        ident = sb("ident", [P, P])
        identb = sb("identb", [P, P], bf16)
        mean = sb("mean", [C, C])
        konst = sb("konst", [P, 2])
        EPS, SPM = konst[:, 0:1], konst[:, 1:2]

        g3 = sb("g3", [P, BLK, 3 * E], bf16)
        gT = sb("gT", [3 * E, CH], bf16)
        xp = sb("xp", [C, CH])
        hid = sb("hid", [P, HT, CH])
        x2p = sb("x2p", [C, CH])
        xc = sb("xc", [C, CH])
        sq = sb("sq", [C, CH])
        xnp = sb("xnp", [C, CH])

        win = sb("win", [C + 1, 2, WIN])
        xr = [sb("xr0", [P, 2, CH]), sb("xr1", [DR, 2, CH])]
        S = sb("S", [P, 3, CH])
        spl = sb("spl", [P, 3, 3, CH], bf16)
        pk = sb("pk", [3 * GRP, 2, 2, NG, CH], bf16)
        bB = sb("bB", [P, 2, CH])
        cC = sb("cC", [P, 2, CH])
        dA = sb("dA", [P, 6, CH])
        h = sb("h", [P, 8, CH])
        hc = sb("hc", [P, 8, CH])
        carry = sb("carry", [P, NT])
        ys0 = sb("ys0", [P, PIX])
        ys1 = sb("ys1", [P, PIX // 2])
        yr0 = sb("yr0", [P, CH])
        yr1 = sb("yr1", [P, CH])
        sz0 = sb("sz0", [P, 2, CH])
        sz1 = sb("sz1", [P, CH])
        xf = sb("xf", [C, CH])
        ob = sb("ob", [C, CH])
        NA, NH = 6, 8

        ps = [ctx.enter_context(nc.psum_tensor(f"ps{i}", [P, CH], f32)) for i in range(8)]
        p_dt, p_dtx, p_y, p_w = ps[0:2], ps[2:4], ps[4:6], ps[6:8]

        s_ld = sem("weights_loaded")
        s_cst = sem("setup_vector")
        s_setup_pe = sem("setup_tensor")
        s_setup_act = sem("setup_scalar")
        s_ready = sem("setup_done")
        s_xl = [sem("router_x_loaded0"), sem("router_x_loaded1")]
        s_rt = sem("router_logits")
        s_rc = sem("router_copied")
        s_gm = sem("gate_math")
        s_ge = sem("gate_exp")
        s_pad = sem("padding_stored")
        s_dt = sem("dt_broadcast")
        s_exp = sem("dA_ready")
        s_dtx = sem("dtx_broadcast")
        s_mul = sem("dBx_ready")
        s_scan = sem("h_ready")
        s_hc = sem("hC_ready")
        s_carry = sem("carry_ready")
        s_y = sem("y_summed")
        s_ev = sem("y_evacuated")
        s_pr = [sem("work_bank0_ready"), sem("work_bank1_ready")]
        s_pf = [sem("work_bank0_free"), sem("work_bank1_free")]
        s_sp = sem("softplus_steps")
        s_s = sem("dtx_ready")
        s_cast = sem("split_cast")
        s_r1 = sem("split_rest")
        s_lo = sem("split_low")
        s_pk = sem("packed")
        s_win = [sem("window0_loaded"), sem("window1_loaded")]
        s_xp = sem("piece_loaded")
        s_sqr = sem("ln_square")
        s_rs = sem("ln_rstd")
        s_xn = sem("ln_done")
        s_x2s = sem("x2_stored")
        s_xns = sem("xn_stored")
        s_fin = sem("gated_y")
        s_xf = sem("residual_loaded")
        s_out = sem("out_stored")

        PKB = 16 * 24

        block = ctx.enter_context(nc.Block())


        def body_number(img, q, rev, odd):
            return img * BODIES + q * 2 + (NCH * rev + odd)

        def piece_number(img, q, rev):
            return NCH + img * NCH + q + (NCH // 2) * rev

        def next_image(img):
            return (img + 1) % IMGS

        @block.sync
        def _(sp):
            def wait_then_address(semaphore, value):
                sp.wait_ge(s_ld, 16 * N_LOADS)
                sp.wait_ge(semaphore, value)

            loads = [
                (w1[:, :], A["w1T"]), (w2[:, :, :], A["w2T"]), (b1[:, :], A["b1"]), (b2f[:, :], A["b2"]),
                (wr[:, :], A["wrT"]), (w_in[:, :], A["w_in"]), (gam[:, :], A["gamma"]), (bet[:, :], A["beta"]),
                (cb[0][:, :], A["conv_b"][0:P, :]), (cb[1][:, :], A["conv_b"][P:DI, :]),
                (wx[0][:, :], A["w_x"][0:P, :]), (wx[1][:, :], A["w_x"][P:DI, :]), (wxT[:, :], A["w_xT"]),
                (wdt[:, :], A["w_dt"]), (bd[0][:, :], A["b_dt"][0:P, :]), (bd[1][:, :], A["b_dt"][P:DI, :]),
                (amat[:, :], A["a_log"]), (dvec[0][:, :], A["d"][0:P, :]), (dvec[1][:, :], A["d"][P:DI, :]),
                (wo0[:, :], A["w_out"][0:P, :]), (wo1[0:DR, :], A["w_out"][P:DI, :]), (wo1[DR:P, :], A["w_out"][P:DI, :]),
                (red[:, :, :], A["c_red"].rearrange("p (r c) -> p r c", r=4)), (ident[:, :], A["c_ident"]),
                (mean[:, :], A["c_mean"]),
                (hid[0:3 * GRP, 0, :], A["c_sel"]),
                (hid[0:3 * E, 1, :], A["c_gate"][:, 0:CH]), (hid[0:3 * E, 2, 0:HT * P - CH], A["c_gate"][:, CH:HT * P]),
                (scl[:, :], A["scale"].partition_broadcast(P)), (rb[:, :], A["router_b"].partition_broadcast(P)),
                (ys0[0:C + 1, 0:TAPS * DI], A["conv_w"].partition_broadcast(C + 1)),
            ]
            for credit in (s_x2s, s_xns, s_out):
                sp.sem_inc(credit, 16)
            for out, src in loads:
                sp.dma_start(out, src).then_inc(s_ld, 16)
            assert len(loads) == N_LOADS
            HALF = PIX // 2
            with sp.Fori(0, IMGS) as i:
                for half in range(2):
                    wait_then_address(s_rt, i * 2 + half + 1)
                    sp.dma_start(hc[0:C, 4 * half:4 * half + 4, :],
                                 A["x"][bass.ds(i, 1), :, half * HALF:(half + 1) * HALF].rearrange("o c (a t) -> (o c) a t", a=4)
                                 ).then_inc(s_xl[half], 16)
            sp.wait_ge(s_ready, 1)
            for i in range(IMGS):
                sp.dma_start(xn_d[i, :, 0:TAPS - 1], ys0[0:C + 1, 1024:1024 + TAPS - 1]).then_inc(s_pad, 16)
                sp.dma_start(xn_d[i, :, PADW - (TAPS - 1):PADW], ys0[0:C + 1, 1024:1024 + TAPS - 1]).then_inc(s_pad, 16)
                for k in range(PIX // 1024):
                    sp.dma_start(xn_d[i, C:C + 1, TAPS - 1 + 1024 * k:TAPS - 1 + 1024 * (k + 1)],
                                 ys0[0:1, 2048:3072]).then_inc(s_pad, 16)

            def load_piece(image, j, pc):
                wait_then_address(s_xn, pc + 1)
                sp.dma_start(xp[:, :], A["x"][bass.ds(image, 1), :, bass.ds(j * CH, CH)].rearrange("o c t -> (o c) t")).then_inc(s_xp, 16)

            def store_x2(image, j, pc, u):
                bank, at = u.at["Y2"]
                wait_then_address(s_pf[bank], at + 2)
                sp.dma_start(x2_d[bass.ds(image, 1), :, bass.ds(j * CH, CH)].rearrange("o c t -> (o c) t"), x2p[:, :]).then_inc(s_x2s, 16)

            def store_xn(image, j, pc):
                wait_then_address(s_xn, pc + 2)
                sp.dma_start(xn_d[bass.ds(image, 1), 0:C, bass.ds(TAPS - 1 + j * CH, CH)].rearrange("o c t -> (o c) t"), xnp[:, :]).then_inc(s_xns, 16)

            def load_window(image, chunk, par, pieces):
                if pieces is not None:
                    wait_then_address(s_xns, pieces * 16 + 16)
                sp.dma_start(win[:, par, :], xn_d[bass.ds(image, 1), :, bass.ds(chunk * CH, WIN)].rearrange("o c t -> (o c) t")).then_inc(s_win[par], 16)

            def pack(part, par):
                rows = slice(GRP * part, GRP * part + GRP)
                for g in range(4):
                    sp.dma_start(pk[rows, par, :, g, :], spl[GRP * g:GRP * g + GRP, part, 0:2, :]).then_inc(s_pk, 16)
                for k in range(4):
                    sp.dma_start(pk[rows, par, k // 2, 4 + k % 2, :], spl[GRP * k:GRP * k + GRP, part, 2, :]).then_inc(s_pk, 16)

            with sp.Fori(0, NCH) as j:
                base = [j * count(PRO_PIECE, i) + count(bank_uses(False, False, False, prep=False), i) for i in (0, 1)]
                load_piece(0, j, j)
                store_x2(0, j, j, Uses(bank_uses(True, False, False, prep=False), base))
                store_xn(0, j, j)
            sp.wait_ge(s_pad, 16 * (2 + PIX // 1024) * IMGS)
            for c in range(2):
                load_window(0, c, c, NCH)
            sp.wait_ge(s_cast, 1)
            pack(0, 0)
            sp.wait_ge(s_cast, 2)
            pack(1, 0)
            sp.wait_ge(s_lo, 2)
            pack(2, 0)

            def store_out(img, chunk, at):
                wait_then_address(s_pf[1], at + 2)
                sp.dma_start(A["out"][bass.ds(img, 1), :, bass.ds(chunk * CH, CH)].rearrange("o c t -> (o c) t"), ob[:, :]).then_inc(s_out, 16)

            def load_residual(img, chunk, f):
                wait_then_address(s_x2s, (img + 1) * (NCH * 16) + 16)
                sp.dma_start(xf[:, :], x2_d[bass.ds(img, 1), :, bass.ds(chunk * CH, CH)].rearrange("o c t -> (o c) t")).then_inc(s_xf, 16)

            def body(img, q, rev, odd, last, fin, u):
                n, pc = body_number(img, q, rev, odd), piece_number(img, q, rev)
                par, j = odd, q + (NCH // 2) * rev
                nimg = next_image(img)
                if last and rev:
                    pass
                elif last:
                    load_window(img, NCH - 1 - odd, par, None)
                else:
                    load_window(img, chunk_of(q, rev, odd) + (-2 if rev else 2), par, None if rev else (img + 1) * NCH)
                if not odd:
                    load_piece(nimg, j, pc)
                if fin:
                    load_residual(img, chunk_of(q, rev, odd) + 1, None)
                if last and rev:
                    sp.wait_ge(s_xns, ((img + 1) * NCH + (NCH // 2)) * 16 + 16)
                sp.wait_ge(s_cast, 2 * n + 3)
                pack(0, 1 - par)
                if last and rev:
                    load_window(nimg, odd, par, None)
                if fin:
                    store_out(img, chunk_of(q, rev, odd) + 1, u.at["OUT"][1])
                sp.wait_ge(s_cast, 2 * n + 4)
                pack(1, 1 - par)
                sp.wait_ge(s_lo, n + 3)
                pack(2, 1 - par)
                if odd:
                    store_x2(nimg, j, pc, u)
                    store_xn(nimg, j, pc)

            def tail(img, u):
                load_residual(img, 0, None)
                store_out(img, 0, u.at["OUT"][1])

            bodies(sp, body, tail)
            sp.wait_ge(s_out, 16 * IMGS * NCH + 16)
            sp.wait_ge(s_x2s, 16 * NCH * (IMGS + 1) + 16)
            sp.wait_ge(s_xns, 16 * NCH * (IMGS + 1) + 16)
            for k in range(2):
                sp.wait_ge(s_win[k], 16 * (IMGS * BODIES // 2 + 1))
            sp.wait_ge(s_pk, PKB * (IMGS * BODIES + 1))

        @block.tensor
        def _(pe):
            mm = nc.tensor.matmul
            pe.wait_ge(s_ld, 16 * N_LOADS)
            mm(ps[0][0:1, 0:2 * DI], bet[:, :], w_in[:, :], start=True, stop=True).then_inc(s_setup_pe, 1)
            mm(ps[1][:, 0:DI], wxT[:, 0:P], wdt[:, :], start=True, stop=True).then_inc(s_setup_pe, 1)
            mm(ps[2][0:DR, 0:DI], wxT[:, P:DI], wdt[:, :], start=True, stop=True).then_inc(s_setup_pe, 1)
            pe.sem_inc(s_rt, 2)
            with pe.Fori(0, IMGS) as i:
                for half in range(2):
                    pe.wait_ge(s_xl[half], i * 16 + 16)
                    pe.wait_ge(s_rc, i * 2 + half + 1)
                    for b in range(16):
                        last = mm(ps[6 + half][:, E * b:E * b + E], hc[0:C, 4 * half + b // 4, P * (b % 4):P * (b % 4) + P],
                                  wr[:, :], start=True, stop=True)
                    last.then_inc(s_rt, 1)

            def begin(u, name):
                bank, at = u.at[name]
                pe.wait_ge(s_pf[bank], at + 1)
                return p_w[bank]

            def ready(u, name, last):
                last.then_inc(s_pr[u.at[name][0]], 1)

            def gates_transposed(image, j, u):
                out = begin(u, "GT")
                for s in range(4):
                    last = mm(out[0:3 * E, P * s:P * s + P],
                              g3[:, bass.ds(image * (PIX // P) + (j * 4 + s), 1), :].rearrange("p o e -> p (o e)"),
                              identb[:, :], start=True, stop=True)
                ready(u, "GT", last)

            def hidden(m, pc, u):
                if m == 0:
                    pe.wait_ge(s_xp, pc * 16 + 16)
                ready(u, f"H{m}", mm(begin(u, f"H{m}")[:, :], w1[:, P * m:P * m + P], xp[:, :], start=True, stop=True))

            def gate_rows(m, u):
                if m == 0:
                    pe.wait_ge(s_pf[1], u.at["GT"][1] + 2)
                ready(u, f"G{m}", mm(begin(u, f"G{m}")[:, :], gsel[:, m, :], gT[:, :], start=True, stop=True))

            def expert_out(m, u, prev):
                if m == 0:
                    begin(u, "Y2")
                bank, at = prev.at[f"G{m}"]
                pe.wait_ge(s_pf[bank], at + 2)
                mm(p_w[0][0:C, :], w2[:, m, :], hid[:, m, :], start=(m == 0), stop=False)

            def expert_bias(u):
                for s in range(3):
                    last = mm(p_w[0][0:C, :], b2s[:, s, :], gT[:, :], start=False, stop=(s == 2))
                ready(u, "Y2", last)

            def ln_mean(u):
                pe.wait_ge(s_pf[0], u.at["Y2"][1] + 2)
                ready(u, "MU", mm(begin(u, "MU")[0:C, :], mean[:, :], x2p[:, :], start=True, stop=True))

            def ln_var(pc, u):
                pe.wait_ge(s_sqr, pc + 1)
                ready(u, "VAR", mm(begin(u, "VAR")[0:C, :], mean[:, :], sq[:, :], start=True, stop=True))

            def project(half, first, k, par, rev, u):
                name, lo, m = f"U{half}", P * half, (P, DR)[half]
                if first:
                    begin(u, name)
                for t in (k, k + 1):
                    at = 2 * (TAPS - 1) - t if rev else t
                    last = mm(p_w[half][0:m, :], w_u[:, t, lo:lo + m], win[:, par, at:at + CH],
                              start=(t == 0), stop=(t == TAPS - 1))
                if not first:
                    ready(u, name, last)

            def project_z(half, par, u):
                lo, m = DI + P * half, (P, DR)[half]
                ready(u, f"Z{half}", mm(begin(u, f"Z{half}")[0:m, :], w_g[:, lo:lo + m], win[:, par, TAPS - 1:TAPS - 1 + CH],
                                        start=True, stop=True))

            def from_xr(name, w0, w1_, m, par, u, halves):
                out = begin(u, name)
                if name == "D0":
                    for b, use in enumerate(("U0", "U1")):
                        pe.wait_ge(s_pf[b], u.at[use][1] + 2)
                mm(out[0:m, :], w0, xr[0][:, par, :], start=True, stop=False)
                ready(u, name, mm(out[0:m, :], w1_, xr[1][:, par, :], start=False, stop=True))

            def project_dt(half, par, u):
                lo, m = P * half, (P, DR)[half]
                from_xr(f"D{half}", w_d[0][:, lo:lo + m], w_d[1][:, lo:lo + m], m, par, u, None)

            def bc(which, dst, i, par):
                ch, r, _ = TILES[i]
                return mm(dst[:, :], sel[:, r, :], pk[:, par, which, ch // GRP, :], start=True, stop=True)

            def bc_dt(n, i, par):
                if i == 0:
                    pe.wait_ge(s_pk, (n + 1) * PKB)
                pe.wait_ge(s_exp, n * NT + (i + 1))
                bc(0, p_dt[i % 2], i, par).then_inc(s_dt, 1)

            def bc_dtx(n, i, par):
                pe.wait_ge(s_scan, n * NT + (i - 1 + 8))
                bc(1, p_dtx[i % 2], i, par).then_inc(s_dtx, 1)

            def sum_states(n, r, par):
                top = r < NT0 // BATCH
                dst = p_y[0 if top else 1]
                if r in (0, NT0 // BATCH):
                    pe.wait_ge(s_ev, n * 2 + (1 if top else 2))
                    mm(dst[:, :], diag[0 if top else 1][:, :], xr[0 if top else 1][:, par, :], start=True, stop=False,
                       skip_group_check=True)
                pe.wait_ge(s_hc, n * NT + (BATCH * (r + 1) + 8))
                for i in range(BATCH * r, BATCH * r + BATCH):
                    _, row, col = TILES[i]
                    last = mm(dst[GRP * col:GRP * col + GRP, :], red[:, row, :], hc[:, i % NH, :], start=False,
                              stop=(row == 3), skip_group_check=True)
                last.then_inc(s_y, 1)

            def finish(u, half, f):
                pe.wait_ge(s_fin, f * 4 + 4)
                out = begin(u, "OUT")
                mm(out[0:C, :], wo0[:, :], yr0[:, :], start=True, stop=False)
                lo = DR * half
                ready(u, "OUT", mm(out[0:C, :], wo1[lo:lo + DR, :], yr1[lo:lo + DR, :], start=False, stop=True))

            pe.wait_ge(s_ready, 1)
            with pe.Fori(0, NCH) as j:
                base = [j * count(PRO_PIECE, i) for i in (0, 1)]
                ua = Uses(bank_uses(False, False, False, prep=False), base)
                base = [base[i] + count(bank_uses(False, False, False, prep=False), i) for i in (0, 1)]
                ub = Uses(bank_uses(True, False, False, prep=False), base)
                gates_transposed(0, j, ua)
                for m in range(HT):
                    hidden(m, j, ua)
                for m in range(HT):
                    gate_rows(m, ua)
                for m in range(HT):
                    expert_out(m, ub, ua)
                expert_bias(ub)
                ln_mean(ub)
                ln_var(j, ub)
            up = Uses(PRO_PREP, [NCH * count(PRO_PIECE, i) for i in (0, 1)])
            pe.wait_ge(s_win[0], 16)
            for half in range(2):
                project(half, True, 0, 0, 0, up)
                project(half, False, 2, 0, 0, up)
            project_dt(0, 0, up)
            project_dt(1, 0, up)
            from_xr("B", w_b[0][:, :], w_b[1][:, :], P, 0, up, None)
            from_xr("C", w_c[0][:, :], w_c[1][:, :], P, 0, up, None)
            for i in range(LEAD_DT):
                bc_dt(0, i, 0)
            for i in range(LEAD_DTX):
                bc_dtx(0, i, 0)

            even = [None]

            def body(img, q, rev, odd, last, fin, u):
                n, pc = body_number(img, q, rev, odd), piece_number(img, q, rev)
                par, nxt, j = odd, 1 - odd, q + (NCH // 2) * rev
                nrev = (rev == 1) != (last and odd == 1)
                nimg = next_image(img)
                prev, even[0] = even[0], u
                for i in range(NT):
                    if i + LEAD_DT < NT:
                        bc_dt(n, i + LEAD_DT, par)
                    else:
                        bc_dt(n + 1, i + LEAD_DT - NT, nxt)
                    if i == 0:
                        pe.wait_ge(s_win[nxt], (img * (BODIES // 2) + q + (NCH // 2) * rev + 1 + odd) * 16)
                    if i < 4:
                        project(i // 2, i % 2 == 0, 2 * (i % 2), nxt, nrev, u)
                    if i == 4 and nrev:
                        project_z(0, nxt, u)
                        project_z(1, nxt, u)
                    if i == 6:
                        project_dt(0, nxt, u)
                    if i == 7:
                        project_dt(1, nxt, u)
                    if i == 9:
                        from_xr("B", w_b[0][:, :], w_b[1][:, :], P, nxt, u, None)
                    if i == 10:
                        from_xr("C", w_c[0][:, :], w_c[1][:, :], P, nxt, u, None)
                    if i == 11 and fin:
                        finish(u, odd, img * NCH + q * 2 + odd - 1)
                    if not odd:
                        if i == 12:
                            gates_transposed(nimg, j, u)
                        if i in (13, 15, 17):
                            hidden(i - 13, pc, u)
                            hidden(i - 12, pc, u)
                        if i in (19, 20, 21):
                            gate_rows(2 * (i - 19), u)
                            gate_rows(2 * (i - 19) + 1, u)
                    else:
                        if i in (12, 13, 14):
                            expert_out(2 * (i - 12), u, prev)
                            expert_out(2 * (i - 12) + 1, u, prev)
                        if i == 15:
                            expert_bias(u)
                        if i == 17:
                            ln_mean(u)
                        if i == 20:
                            ln_var(pc, u)
                    if i + LEAD_DTX < NT:
                        bc_dtx(n, i + LEAD_DTX, par)
                    else:
                        bc_dtx(n + 1, i + LEAD_DTX - NT, nxt)
                    if i % BATCH == 1 and i > 4:
                        sum_states(n, i // BATCH - 1, par)
                sum_states(n, NB - 1, par)

            def tail(img, u):
                finish(u, 0, img * NCH + (NCH - 1))

            bodies(pe, body, tail)

        @block.scalar
        def _(act):
            A_ = nc.scalar.activation
            act.sem_inc(s_exp, 2)
            act.sem_inc(s_ev, 2)
            act.sem_inc(s_pf[0], 1)
            act.sem_inc(s_pf[1], 1)
            act.wait_ge(s_setup_pe, 3)
            A_(w_g[C:C + 1, :], ps[0][0:1, 0:2 * DI], ACT.Copy).then_inc(s_setup_act, 1)
            A_(w_d[0][:, :], ps[1][:, 0:DI], ACT.Copy).then_inc(s_setup_act, 1)
            A_(w_d[1][:, :], ps[2][0:DR, 0:DI], ACT.Copy).then_inc(s_setup_act, 1)
            A_(amat[:, :], amat[:, :], ACT.Exp).then_inc(s_setup_act, 1)
            act.wait_ge(s_gm, 1)
            A_(dA[:, 0:2, :], dA[:, 0:2, :], ACT.Exp).then_inc(s_ge, 1)
            act.wait_ge(s_ready, 1)

            def begin(u, name):
                bank, at = u.at[name]
                act.wait_ge(s_pr[bank], at + 1)
                return p_w[bank]

            def free(u, name, ins):
                ins.then_inc(s_pf[u.at[name][0]], 1)

            def main_tables():
                nc.scalar.preload_act_table_set("natural_log_exp_and_others")

            def copy_gates(u):
                free(u, "GT", A_(gT[:, :], begin(u, "GT")[0:3 * E, :], ACT.Copy))

            def gelu(ms, u):
                for m in ms:
                    free(u, f"H{m}", A_(hid[:, m, :], begin(u, f"H{m}")[:, :], ACT.Gelu, bias=b1[:, m:m + 1]))
                main_tables()

            def ln_square(u, pc):
                act.wait_ge(s_pf[1], u.at["MU"][1] + 2)
                A_(sq[:, :], xc[:, :], ACT.Square).then_inc(s_sqr, 1)

            def ln_rstd(u, pc):
                out = begin(u, "VAR")
                free(u, "VAR", A_(sq[:, :], out[0:C, :], ACT.Ln, bias=EPS[0:C, :]))
                act.wait_ge(s_pf[0], u.at["VAR"][1] + 2)
                A_(sq[:, :], sq[:, :], ACT.Exp, scale=-0.5).then_inc(s_rs, 1)

            def silus(u, par, nrev, cpar, f):
                for k, m in enumerate((P, DR)):
                    free(u, f"U{k}", A_(xr[k][:, par, :], begin(u, f"U{k}")[0:m, :], ACT.Silu, bias=cb[k][:, :]))
                if nrev:
                    if f is not None:
                        act.wait_ge(s_fin, f * 4 + 4)
                    free(u, "Z0", A_(sz0[:, cpar, :], begin(u, "Z0")[:, :], ACT.Silu))
                    free(u, "Z1", A_(sz1[DR * cpar:DR * cpar + DR, :], begin(u, "Z1")[0:DR, :], ACT.Silu))
                main_tables()

            def softplus(u, b):
                v = (S[:, 0, :], S[0:DR, 2, :])
                act.wait_ge(s_lo, b + 1)
                for k, m in enumerate((P, DR)):
                    A_(v[k], begin(u, f"D{k}")[0:m, :], ACT.Relu, bias=nbd[k][:, :], scale=-1.0).then_inc(s_sp, 1)
                for k, m in enumerate((P, DR)):
                    act.wait_ge(s_sp, b * 6 + (1 + k))
                    A_(v[k], v[k], ACT.Exp, bias=SPM[0:m, :], scale=-1.0).then_inc(s_sp, 1)
                for k in range(2):
                    act.wait_ge(s_sp, b * 6 + (3 + k))
                    A_(v[k], v[k], ACT.Ln, bias=1.0).then_inc(s_sp, 1)

            def copy_b(u, par):
                free(u, "B", A_(bB[:, par, :], begin(u, "B")[:, :], ACT.Copy))

            def copy_c(u, par):
                free(u, "C", A_(cC[:, par, :], begin(u, "C")[:, :], ACT.Copy))

            def cast_high(b):
                act.wait_ge(s_s, b * 2 + 2)
                if not isinstance(b, int):
                    act.wait_ge(s_pk, b * PKB)
                A_(spl[:, 0, :, :], S[:, :, :], ACT.Copy).then_inc(s_cast, 1)

            def cast_mid(b):
                act.wait_ge(s_r1, b + 2)
                A_(spl[:, 1, :, :], S[:, :, :], ACT.Copy).then_inc(s_cast, 1)

            def exp_dA(n, i):
                act.wait_ge(s_dt, n * NT + (i + 1))
                act.wait_ge(s_scan, n * NT + (i - NA + 1 + 8))
                col = TILES[i][0] // CPT
                A_(dA[:, i % NA, :], p_dt[i % 2][:, :], ACT.Exp, scale=amat[:, col:col + 1]).then_inc(s_exp, 1)

            def evacuate(n, half, rev, odd, chunk, u, fin):
                act.wait_ge(s_y, n * NB + (2 + (NB if half else NT0 // BATCH)))
                if fin:
                    act.wait_ge(s_pf[1], u.at["OUT"][1] + 2)
                src, lo = (p_y[1][0:DR, :], DR * (odd ^ rev)) if half else (p_y[0][:, :], 0)
                rows = slice(lo, lo + DR) if half else slice(0, P)
                if rev:
                    dst = (yr1 if half else yr0)[rows, :]
                elif half:
                    dst = ys1[rows, bass.ds(chunk, CH)]
                else:
                    dst = ys0[:, bass.ds(chunk, CH)]
                A_(dst, src, ACT.Copy).then_inc(s_ev, 1)

            with act.Fori(0, NCH) as j:
                base = [j * count(PRO_PIECE, i) for i in (0, 1)]
                ua = Uses(bank_uses(False, False, False, prep=False), base)
                base = [base[i] + count(bank_uses(False, False, False, prep=False), i) for i in (0, 1)]
                ub = Uses(bank_uses(True, False, False, prep=False), base)
                copy_gates(ua)
                gelu(range(HT), ua)
                ln_square(ub, j)
                ln_rstd(ub, j)
            up = Uses(PRO_PREP, [NCH * count(PRO_PIECE, i) for i in (0, 1)])
            silus(up, 0, False, 0, None)
            softplus(up, 0)
            copy_b(up, 0)
            copy_c(up, 0)
            cast_high(0)
            cast_mid(0)
            for i in range(LEAD_DT):
                exp_dA(0, i)

            def body(img, q, rev, odd, last, fin, u):
                n, pc = body_number(img, q, rev, odd), piece_number(img, q, rev)
                nxt = 1 - odd
                nrev = (rev == 1) != (last and odd == 1)
                cpar = 1 - nxt
                f = img * NCH + q * 2 + odd - 1 if fin else None
                for i in range(NT):
                    exp_dA(*((n, i + LEAD_DT) if i + LEAD_DT < NT else (n + 1, i + LEAD_DT - NT)))
                    if i == 4:
                        silus(u, nxt, nrev, cpar, f)
                    if i == 8:
                        softplus(u, n + 1)
                    if i == 10:
                        copy_b(u, nxt)
                    if i == 11:
                        copy_c(u, nxt)
                        cast_high(n + 1)
                    if i == 13:
                        cast_mid(n + 1)
                    if not odd:
                        if i == 12:
                            copy_gates(u)
                        if i in (14, 16, 18):
                            gelu((i - 14, i - 13), u)
                    else:
                        if i == 19:
                            ln_square(u, pc)
                        if i == 21:
                            ln_rstd(u, pc)
                    if i == 19:
                        evacuate(n, 0, rev, odd, q * (2 * CH) + odd * CH, u, fin)
                evacuate(n, 1, rev, odd, q * CH, u, fin)

            def tail(img, u):
                pass

            bodies(act, body, tail)

        @block.vector
        def _(dve):
            V = nc.vector
            dve.sem_inc(s_scan, 8)
            dve.sem_inc(s_rc, 2)
            step = [0]

            def link(ins):
                step[0] += 1
                ins.then_inc(s_cst, 1)
                dve.wait_ge(s_cst, step[0])

            dve.wait_ge(s_ld, 16 * N_LOADS)
            link(V.memset(konst[:, 0:1], LN_EPS))
            link(V.memset(yr1[:, :], 0.0))
            link(V.memset(sz1[:, :], 0.0))
            link(V.memset(konst[:, 1:2], SP_MAX))
            link(V.tensor_copy(sel[:, :, :], hid[0:3 * GRP, 0, :].rearrange("p (r c) -> p r c", r=4)))
            link(V.tensor_copy(gsel[:, 0:4, :], hid[0:3 * E, 1, :].rearrange("p (r c) -> p r c", r=4)))
            link(V.tensor_copy(gsel[:, 4:6, :], hid[0:3 * E, 2, 0:2 * P].rearrange("p (r c) -> p r c", r=2)))
            link(V.tensor_copy(identb[:, :], ident[:, :]))
            link(V.tensor_scalar(w2[:, :, :], w2[:, :, :], scl[:, :], None, ALU.mult))
            link(V.tensor_scalar(b2f[:, :], b2f[:, :], scl[0:3 * E, :], None, ALU.mult))
            link(V.tensor_copy(b2s[:, 0, :], b2f[:, :]))
            link(V.tensor_tensor(b2r[:, :], b2f[:, :], b2s[:, 0, :], ALU.subtract))
            link(V.tensor_copy(b2s[:, 1, :], b2r[:, :]))
            link(V.tensor_tensor(b2s[:, 2, :], b2r[:, :], b2s[:, 1, :], ALU.subtract))
            link(V.tensor_scalar(w_g[0:C, :], w_in[:, :], gam[:, :], None, ALU.mult))
            link(V.tensor_scalar(wo0[:, :], wo0[:, :], 0.5, None, ALU.mult))
            link(V.tensor_scalar(wo1[:, :], wo1[:, :], 0.5, None, ALU.mult))
            for k in range(2):
                m = (P, DR)[k]
                link(V.tensor_scalar(nbd[k][:, :], bd[k][:, :], -1.0, SP_MAX, ALU.mult, ALU.add))
                link(V.tensor_scalar(diag[k][:, :], ident[0:m, :], dvec[k][:, :], None, ALU.mult))
                for w, lo in ((w_b[k], RANK), (w_c[k], RANK + NST)):
                    link(V.tensor_copy(w[:, :].rearrange("p (c s) -> p c s", c=CPT),
                                       wx[k][:, lo:lo + NST].unsqueeze(1).to_broadcast([m, CPT, NST])))
            dve.wait_ge(s_setup_act, 4)
            link(V.tensor_scalar(amat[:, :], amat[:, :], -1.0, None, ALU.mult))
            cw = ys0[0:C + 1, 0:TAPS * DI].rearrange("p (k c) -> p k c", k=TAPS)
            for k in range(TAPS):
                link(V.tensor_tensor(w_u[:, k, :], w_g[:, 0:DI], cw[:, k, :], ALU.mult))
            link(V.memset(ys0[0:C + 1, 1024:1024 + TAPS - 1], 0.0))
            link(V.memset(ys0[0:1, 2048:3072], 1.0))

            lg = dA[:, 2:4, :].rearrange("p a t -> p (a t)").rearrange("p (b e) -> p b e", e=E)
            with dve.Fori(0, IMGS) as i:
                for half in range(2):
                    dve.wait_ge(s_rt, i * 2 + half + 3)
                    V.tensor_tensor(lg[:, bass.ds(i * 32 + 16 * half, 16), :],
                                    ps[6 + half][:, 0:16 * E].rearrange("p (b e) -> p b e", e=E),
                                    rb[:, :].unsqueeze(1).to_broadcast([P, 16, E]), ALU.add).then_inc(s_rc, 1)
            dve.wait_ge(s_rc, 2 + 2 * IMGS)

            def tmp(a, b):
                return h[:, a:b, :].rearrange("p a t -> p (a t)").rearrange("p (b e) -> p b e", e=E)

            rank, cmp_, gate = tmp(0, 2), tmp(2, 4), tmp(4, 6)
            eg = dA[:, 0:2, :].rearrange("p a t -> p (a t)").rearrange("p (b e) -> p b e", e=E)
            mx = h[:, 6, 0:BLK]
            link(V.memset(rank, 0.0))
            for j in range(E):
                lj = lg[:, :, j:j + 1]
                if j > 0:
                    link(V.tensor_tensor(cmp_[:, :, 0:j], lj.to_broadcast([P, BLK, j]), lg[:, :, 0:j], ALU.is_gt))
                    link(V.tensor_tensor(rank[:, :, 0:j], rank[:, :, 0:j], cmp_[:, :, 0:j], ALU.add))
                if j < E - 1:
                    k = E - 1 - j
                    link(V.tensor_tensor(cmp_[:, :, j + 1:E], lj.to_broadcast([P, BLK, k]), lg[:, :, j + 1:E], ALU.is_ge))
                    link(V.tensor_tensor(rank[:, :, j + 1:E], rank[:, :, j + 1:E], cmp_[:, :, j + 1:E], ALU.add))
            link(V.tensor_scalar(rank, rank, 1.5, None, ALU.is_lt))
            link(V.reduce_max(mx, lg, AX.X))
            V.tensor_tensor(eg, lg, mx.unsqueeze(2).to_broadcast([P, BLK, E]), ALU.subtract).then_inc(s_gm, 1)
            dve.wait_ge(s_ge, 1)
            link(V.tensor_tensor(gate, eg, rank, ALU.mult))
            link(V.reduce_sum(mx, gate, AX.X))
            link(V.reciprocal(mx, mx))
            link(V.tensor_tensor(gate, gate, mx.unsqueeze(2).to_broadcast([P, BLK, E]), ALU.mult))
            link(V.tensor_copy(g3[:, :, 0:E], gate))
            link(V.tensor_tensor(gate, gate, g3[:, :, 0:E], ALU.subtract))
            link(V.tensor_copy(g3[:, :, E:2 * E], gate))
            link(V.tensor_tensor(g3[:, :, 2 * E:3 * E], gate, g3[:, :, E:2 * E], ALU.subtract))
            dve.sem_inc(s_ready, 1)

            def begin(u, name):
                bank, at = u.at[name]
                dve.wait_ge(s_pr[bank], at + 1)
                return p_w[bank]

            def free(u, name, ins):
                ins.then_inc(s_pf[u.at[name][0]], 1)

            def gate_hidden(m, u):
                out = begin(u, f"G{m}")
                bank, at = u.at[f"H{m}"]
                dve.wait_ge(s_pf[bank], at + 2)
                free(u, f"G{m}", V.tensor_tensor(hid[:, m, :], out[:, :], hid[:, m, :], ALU.mult))

            def residual(u, pc):
                out = begin(u, "Y2")
                dve.wait_ge(s_xp, pc * 16 + 16)
                dve.wait_ge(s_x2s, pc * 16 + 16)
                free(u, "Y2", V.tensor_tensor(x2p[:, :], out[0:C, :], xp[:, :], ALU.add))

            def centre(u):
                out = begin(u, "MU")
                dve.wait_ge(s_pf[0], u.at["Y2"][1] + 2)
                free(u, "MU", V.scalar_tensor_tensor(xc[:, :], out[0:C, :], -1.0, x2p[:, :], op0=ALU.mult, op1=ALU.add))

            def dt_max(k, u, b):
                m = (P, DR)[k]
                out = begin(u, f"D{k}")
                dve.wait_ge(s_sp, b * 6 + (5 + k))
                v = (S[:, 0, :], S[0:DR, 2, :])[k]
                free(u, f"D{k}", V.scalar_tensor_tensor(v, out[0:m, :], bd[k][:, :], v, op0=ALU.add, op1=ALU.max))

            def dt_x(k, u, par):
                bank, at = u.at[f"D{k}"]
                dve.wait_ge(s_pf[bank], at + 2)
                out, v = ((S[:, 1, :], S[:, 0, :]), (S[DR:P, 2, :], S[0:DR, 2, :]))[k]
                V.tensor_tensor(out, v, xr[k][:, par, :], ALU.mult).then_inc(s_s, 1)

            def scan(n, i, rev, par):
                if i == 0:
                    dve.wait_ge(s_cast, n * 2 + 2)
                dve.wait_ge(s_dtx, n * NT + (i + 1))
                V.tensor_tensor(p_dtx[i % 2][:, :], p_dtx[i % 2][:, :], bB[:, par, :], ALU.mult).then_inc(s_mul, 1)
                if i % BATCH == 0:
                    dve.wait_ge(s_carry, n * NB + (i // BATCH + 5))
                dve.wait_ge(s_exp, n * NT + (i + 1 + 2))
                dve.wait_ge(s_hc, n * NT + (i - NH + 1 + 8))
                dve.wait_ge(s_mul, n * NT + (i + 1))
                a, b, o = dA[:, i % NA, :], p_dtx[i % 2][:, :], h[:, i % NH, :]
                if rev:
                    a, b, o = a[:, ::-1], b[:, ::-1], o[:, ::-1]
                V.tensor_tensor_scan(o, a, b, carry[:, i:i + 1], ALU.mult, ALU.add).then_inc(s_scan, 1)

            def add_residual(u, f):
                out = begin(u, "OUT")
                dve.wait_ge(s_xf, f * 16 + 16)
                dve.wait_ge(s_out, f * 16 + 16)
                free(u, "OUT", V.tensor_tensor(ob[:, :], out[0:C, :], xf[:, :], ALU.add))

            with dve.Fori(0, NCH) as j:
                base = [j * count(PRO_PIECE, i) for i in (0, 1)]
                ua = Uses(bank_uses(False, False, False, prep=False), base)
                base = [base[i] + count(bank_uses(False, False, False, prep=False), i) for i in (0, 1)]
                ub = Uses(bank_uses(True, False, False, prep=False), base)
                for m in range(HT):
                    gate_hidden(m, ua)
                residual(ub, j)
                centre(ub)
            up = Uses(PRO_PREP, [NCH * count(PRO_PIECE, i) for i in (0, 1)])
            for k in range(2):
                dt_max(k, up, 0)
            for k in range(2):
                dt_x(k, up, 0)

            def body(img, q, rev, odd, last, fin, u):
                n, pc = body_number(img, q, rev, odd), piece_number(img, q, rev)
                par, nxt = odd, 1 - odd
                for i in range(NT):
                    if i == 9:
                        dt_max(0, u, n + 1)
                        dt_max(1, u, n + 1)
                    if i == 10:
                        dt_x(0, u, nxt)
                        dt_x(1, u, nxt)
                    if i == 13 and fin:
                        add_residual(u, img * NCH + q * 2 + odd - 1)
                    if not odd:
                        if i in (20, 21, 22):
                            gate_hidden(2 * (i - 20), u)
                            gate_hidden(2 * (i - 20) + 1, u)
                    else:
                        if i == 16:
                            residual(u, pc)
                        if i == 18:
                            centre(u)
                    scan(n, i, rev, par)

            def tail(img, u):
                add_residual(u, img * NCH + (NCH - 1))

            bodies(dve, body, tail)

        @block.gpsimd
        def _(pool):
            G = nc.gpsimd
            pool.sem_inc(s_hc, 8)
            pool.sem_inc(s_r1, 1)
            pool.sem_inc(s_lo, 1)
            pool.sem_inc(s_xn, 1)
            pool.sem_inc(s_y, 2)
            pool.sem_inc(s_carry, NB - 1)
            G.memset(carry[:, :], 0.0).then_inc(s_carry, 1)

            def normalise(pc):
                pool.wait_ge(s_rs, pc + 1)
                pool.wait_ge(s_xns, pc * 16 + 16)
                G.tensor_tensor(xnp[:, :], xc[:, :], sq[:, :], ALU.mult).then_inc(s_xn, 1)

            def split_rest(b):
                pool.wait_ge(s_cast, b * 2 + 1)
                G.tensor_tensor(S[:, :, :], S[:, :, :], spl[:, 0, :, :], ALU.subtract).then_inc(s_r1, 1)

            def split_low(b):
                pool.wait_ge(s_cast, b * 2 + 2)
                G.tensor_tensor(spl[:, 2, :, :], S[:, :, :], spl[:, 1, :, :], ALU.subtract).then_inc(s_lo, 1)

            def gate_y(f, half, chunk, par):
                G.tensor_tensor(yr0[:, :], yr0[:, :], ys0[:, bass.ds(chunk * CH, CH)], ALU.add).then_inc(s_fin, 1)
                G.tensor_tensor(yr1[:, :], yr1[:, :], ys1[:, bass.ds((chunk - half) * (CH // 2), CH)], ALU.add).then_inc(s_fin, 1)
                pool.wait_ge(s_fin, f * 4 + 1)
                G.tensor_tensor(yr0[:, :], yr0[:, :], sz0[:, half, :], ALU.mult).then_inc(s_fin, 1)
                pool.wait_ge(s_fin, f * 4 + 2)
                G.tensor_tensor(yr1[:, :], yr1[:, :], sz1[:, :], ALU.mult).then_inc(s_fin, 1)

            def times_c(n, i, par, reset):
                if i == 0:
                    pool.wait_ge(s_cast, n * 2 + 2)
                pool.wait_ge(s_scan, n * NT + (i + 1 + 8))
                if i % BATCH == 0:
                    pool.wait_ge(s_y, n * NB + (i // BATCH + 1))
                G.tensor_tensor(hc[:, i % NH, :], h[:, i % NH, :], cC[:, par, :], ALU.mult).then_inc(s_hc, 1)
                if i % BATCH == BATCH - 1:
                    cols = carry[:, i - BATCH + 1:i + 1]
                    if reset is None:
                        G.memset(cols, 0.0).then_inc(s_carry, 1)
                    else:
                        s0 = (i - BATCH + 1) % NH
                        G.tensor_copy(cols, h[:, s0:s0 + BATCH, reset]).then_inc(s_carry, 1)

            with pool.Fori(0, NCH) as j:
                normalise(j)
            split_rest(0)
            split_low(0)

            def body(img, q, rev, odd, last, fin, u):
                n, pc = body_number(img, q, rev, odd), piece_number(img, q, rev)
                par = odd
                reset = None if last and odd else (0 if rev else CH - 1)
                for i in range(NT):
                    if i == 1 and fin:
                        pool.wait_ge(s_ready, 1)
                        pool.wait_ge(s_ev, n * 2 + 2)
                        gate_y(img * NCH + q * 2 + odd - 1, odd, chunk_of(q, rev, odd) + 1, 1 - odd)
                    if i == 13:
                        split_rest(n + 1)
                    if i == 15:
                        split_low(n + 1)
                    if i == 23 and odd:
                        normalise(pc)
                    times_c(n, i, par, reset)

            def tail(img, u):
                pool.wait_ge(s_ready, 1)
                pool.wait_ge(s_ev, (img + 1) * (BODIES * 2) + 2)
                gate_y(img * NCH + (NCH - 1), 0, 0, 1)

            bodies(pool, body, tail)


N_LOADS = 31


def kernel(**inputs):
    import concourse.bacc as _bacc
    from concourse.bass_utils import run_bass_kernel_spmd as _run

    a = {k: np.asarray(v) for k, v in inputs.items()}
    L0, L1 = "L0_conv_", "L1_conv_"
    laid = {
        "x": a["x"].reshape(IMGS, C, PIX),
        "w1T": a[L0 + "fc1_w"].transpose(2, 0, 1).reshape(C, E * HID),
        "w2T": a[L0 + "fc2_w"].transpose(0, 2, 1).reshape(HT, P, C).transpose(1, 0, 2),
        "b1": a[L0 + "fc1_b"].reshape(HT, P).T,
        "b2": np.tile(a[L0 + "fc2_b"], (3, 1)),
        "wrT": a[L0 + "router_w"].T,
        "router_b": a[L0 + "router_b"],
        "scale": a[L0 + "scale"],
        "w_in": a[L1 + "W_in"],
        "gamma": a[L1 + "gamma"][:, None],
        "beta": a[L1 + "beta"][:, None],
        "conv_w": a[L1 + "conv_w"].T.reshape(-1),
        "conv_b": a[L1 + "conv_b"][:, None],
        "w_x": a[L1 + "W_xproj"],
        "w_xT": a[L1 + "W_xproj"][:, :RANK].T,
        "w_dt": a[L1 + "W_dt"],
        "b_dt": a[L1 + "b_dt"][:, None],
        "a_log": a[L1 + "A_log"].reshape(NT, P).T,
        "d": a[L1 + "D"][:, None],
        "w_out": a[L1 + "W_out"],
    }
    laid.update(selectors())
    nc = _bacc.Bacc("TRN2", target_bir_lowering=False, num_devices=1)
    arrays, A = {}, {}
    for name, v in laid.items():
        v = np.ascontiguousarray(v)
        arrays[f"in_{name}"] = v
        A[name] = nc.dram_tensor(f"in_{name}", v.shape, mybir.dt.from_np(v.dtype), kind="ExternalInput").ap()
    A["out"] = nc.dram_tensor("out", [IMGS, C, PIX], mybir.dt.float32, kind="ExternalOutput").ap()
    moe_mamba(nc, A)
    r = _run(nc, [arrays], core_ids=[0])
    return r.results[0]["out"].reshape(IMGS, C, 64, 64)
```

```python
import concourse.bass as bass
from concourse import mybir
from contextlib import ExitStack
import numpy as np

IMGS, C, PIX = 8, 96, 4096
E, HID = 4, 192
DI, NST, RANK, TAPS = 192, 16, 6, 4
P = 128
CH = 512
NCH = PIX // CH
NT = DI * NST // P
CPT = P // NST
HT = E * HID // P
GRP = 32
NG = DI // GRP
DR = DI - P
BLK = IMGS * PIX // P
WIN = CH + 2 * (TAPS - 1)
PADW = PIX + 2 * (TAPS - 1)
BODIES = 2 * NCH
LN_EPS = 1e-5
SP_MAX = 40.0
BATCH = 4
NB = NT // BATCH
LEAD_DT, LEAD_DTX = 5, 2
RING = 3

QUART = DR // 4
TILES = [(P + QUART * j + CPT * r, (QUART * j // CPT + r) % 4, r, j) for r in range(QUART // CPT) for j in range(4)]
LOW_BATCHES = len(TILES) // BATCH
TILES += [(GRP * j + CPT * r, r, r, j) for r in range(GRP // CPT) for j in range(4)]

GATES = ([(14, 0), (15, 1), (16, 2)], [(1, 3), (2, 4), (3, 5)])


def ring(odd):
    out = []
    for i in range(NT):
        out += [("gate", m) for slot, m in GATES[odd] if slot == i - 1] + [("tile", i)]
    assert len(out) % RING == 0 and all(kind == "tile" for kind, _ in out[-RING:])
    return out


def selectors():
    sel = np.zeros((3 * GRP, 4, P), np.float32)
    red = np.zeros((P, 4, GRP), np.float32)
    for p in range(P):
        for r in range(4):
            sel[CPT * r + p // NST::GRP, r, p] = 1
            red[p, r, CPT * r + p // NST] = 1
    gate = np.zeros((3 * E, HT, P), np.float32)
    for m in range(HT):
        for p in range(P):
            gate[(m * P + p) // HID::E, m, p] = 1
    return {
        "c_sel": sel.reshape(3 * GRP, -1), "c_red": red.reshape(P, -1), "c_gate": gate.reshape(3 * E, -1),
        "c_ident": np.eye(P, dtype=np.float32), "c_mean": np.full((C, C), 1.0 / C, np.float32),
    }


def bank_uses(odd, next_rev, fin):
    out = [("OUT", 1)] if fin else []
    if not odd:
        return ([("D0", 0), ("GT", 1), ("D1", 1), ("C", 0)] + out + [("H0", 1), ("H1", 0), ("H2", 1), ("U0", 0), ("U1", 1)]
                + ([("Z0", 0)] if next_rev else []) + [("H3", 1), ("H4", 0), ("H5", 1)]
                + ([("Z1", 0)] if next_rev else []))
    return ([("D0", 0), ("D1", 1), ("C", 0)] + out + [("Y2", 1), ("U0", 0), ("MU", 1), ("U1", 1), ("VAR", 0)]
            + ([("Z0", 1), ("Z1", 1)] if next_rev else []))


def count(uses, bank):
    return sum(b == bank for _, b in uses)


class Uses:

    def __init__(self, uses, base):
        self.at, seen = {}, [0, 0]
        for name, bank in uses:
            self.at[name] = (bank, base[bank] + seen[bank])
            seen[bank] += 1


PRO_PIECE = [("GT", 1)] + [(f"H{m}", m % 2) for m in range(HT)] + [("Y2", 1), ("MU", 1), ("VAR", 0)]
PRO_U = [("U0", 0), ("U1", 1)]
PRO_D = [("D0", 0), ("D1", 1), ("C", 0)]
PRO = [count(PRO_PIECE, i) * NCH + 2 * count(PRO_U, i) + count(PRO_D, i) for i in (0, 1)]


def prologue_uses():
    at = [count(PRO_PIECE, i) * NCH for i in (0, 1)]
    out = []
    for uses in (PRO_U, PRO_U, PRO_D):
        out.append(Uses(uses, at))
        at = [at[i] + count(uses, i) for i in (0, 1)]
    return out


def piece_uses(j):
    return Uses(PRO_PIECE, [j * count(PRO_PIECE, i) for i in (0, 1)])


def kinds():
    half = NCH // 2
    return [(0, 0, half - 1, False, False), (0, half - 1, 1, True, False),
            (1, 0, 1, False, False), (1, 1, half - 2, False, True), (1, half - 1, 1, True, True)]


def pair_uses(run):
    rev, _, _, last, fin = run
    return (bank_uses(False, rev == 1, fin), bank_uses(True, (rev == 1) != last, rev == 1))


TAIL = [("OUT", 1)]
PER_IMAGE = [sum(n * (count(a, i) + count(b, i)) for run in kinds() for n in [run[2]] for a, b in [pair_uses(run)])
             + count(TAIL, i) for i in (0, 1)]


def bodies(eng, body, tail):
    with eng.Fori(0, IMGS) as img:
        start = [PRO[i] + img * PER_IMAGE[i] for i in (0, 1)]
        for run in kinds():
            rev, p0, pairs, last, fin = run
            even, odd = pair_uses(run)
            per = [count(even, i) + count(odd, i) for i in (0, 1)]

            def pair(q):
                base = [start[i] + (q - p0) * per[i] for i in (0, 1)]
                body(img, q, rev, 0, last, fin, Uses(even, base))
                base = [base[i] + count(even, i) for i in (0, 1)]
                body(img, q, rev, 1, last, rev == 1, Uses(odd, base))

            if pairs > 1:
                with eng.Fori(p0, p0 + pairs) as q:
                    pair(q)
            else:
                pair(p0)
            start = [start[i] + pairs * per[i] for i in (0, 1)]
        tail(img, Uses(TAIL, start))


def chunk_of(q, rev, odd):
    return (NCH - 1 - odd) - q * 2 if rev else q * 2 + odd


def moe_mamba(nc, A):
    f32, bf16 = mybir.dt.float32, mybir.dt.bfloat16
    ALU, ACT, AX = mybir.AluOpType, mybir.ActivationFunctionType, mybir.AxisListType
    ctx = ExitStack()
    with ctx:
        def sb(name, shape, dt=f32):
            return ctx.enter_context(nc.sbuf_tensor(name, shape, dt))

        def sem(name):
            return ctx.enter_context(nc.semaphore(name))

        xn_d = nc.dram_tensor("xn_d", [IMGS, C + 1, PADW], f32, kind="Internal").ap()
        x2_d = nc.dram_tensor("x2_d", [IMGS, C, PIX], f32, kind="Internal").ap()

        w1 = sb("w1", [C, E * HID])
        w2 = sb("w2", [P, HT, C])
        b1 = sb("b1", [P, HT])
        b2f = sb("b2f", [3 * E, C])
        b2r = sb("b2r", [3 * E, C])
        b2s = sb("b2s", [3 * E, 3, C], bf16)
        scl = sb("scl", [P, 1])
        wr = sb("wr", [C, E])
        rb = sb("rb", [P, E])
        w_in = sb("w_in", [C, DI + 2 * P])
        w_g = sb("w_g", [C + 1, DI + 2 * P])
        gam = sb("gam", [C, 1])
        bet = sb("bet", [C, 1])
        w_u = sb("w_u", [C + 1, TAPS, DI])
        cb = [sb("cb0", [P, 1]), sb("cb1", [DR, 1])]
        wx = [sb("wx0", [P, RANK + 2 * NST]), sb("wx1", [DR, RANK + 2 * NST])]
        wxT = sb("wxT", [RANK, DI])
        wdt = sb("wdt", [RANK, DI])
        w_d = [sb("wd0", [P, 2 * P]), sb("wd1", [DR, 2 * P])]
        w_c = [sb("wc0", [P, P]), sb("wc1", [DR, P])]
        bd = [sb("bd0", [P, 1]), sb("bd1", [DR, 1])]
        nbd = [sb("nbd0", [P, 1]), sb("nbd1", [DR, 1])]
        amat = sb("amat", [P, NT])
        dvec = [sb("dv0", [P, 1]), sb("dv1", [DR, 1])]
        diag = [sb("dg0", [P, P]), sb("dg1", [DR, P])]
        wo0 = sb("wo0", [P, C])
        wo1 = sb("wo1", [P, C])
        sel = sb("sel", [3 * GRP, 4, P], bf16)
        red = sb("red", [P, 4, GRP])
        gsel = sb("gsel", [3 * E, HT, P], bf16)
        ident = sb("ident", [P, P])
        identb = sb("identb", [P, P], bf16)
        mean = sb("mean", [C, C])
        konst = sb("konst", [P, 2])
        EPS, SPM = konst[:, 0:1], konst[:, 1:2]

        g3 = sb("g3", [P, BLK, 3 * E], bf16)
        gT = sb("gT", [3 * E, CH], bf16)
        xp = sb("xp", [C, CH])
        hid = sb("hid", [P, HT, CH])
        x2p = sb("x2p", [C, CH])
        xc = sb("xc", [C, CH])
        sq = sb("sq", [C, CH])
        xnp = sb("xnp", [C, CH])

        win = sb("win", [C + 1, 2, WIN])
        xr = [sb("xr0", [P, 2, CH]), sb("xr1", [DR, 2, CH])]
        S = sb("S", [P, 3, CH])
        spl = sb("spl", [P, 3, 3, CH], bf16)
        pk = sb("pk", [3 * GRP, 2, 2, NG, CH], bf16)
        bB = sb("bB", [P, 2, CH])
        cC = sb("cC", [P, 2, CH])
        dA = sb("dA", [P, 6, CH])
        h = sb("h", [P, 8, CH])
        hc = sb("hc", [P, 8, CH])
        carry = sb("carry", [P, NT])
        ys0 = sb("ys0", [P, PIX])
        ys1 = sb("ys1", [P, PIX])
        yr0 = sb("yr0", [P, CH])
        yr1 = sb("yr1", [P, CH])
        sz0 = sb("sz0", [P, 2, CH])
        sz1 = sb("sz1", [P, 2, CH])
        xf = sb("xf", [C, CH])
        ob = sb("ob", [C, CH])
        NA, NH = 6, 8

        ps = [ctx.enter_context(nc.psum_tensor(f"ps{i}", [P, CH], f32)) for i in range(8)]
        p_dt, p_ring, p_y, p_w = ps[0:2], ps[2:5], ps[5], ps[6:8]

        s_ld = sem("weights_loaded")
        s_cst = sem("setup_vector")
        s_setup_pe = sem("setup_tensor")
        s_setup_act = sem("setup_scalar")
        s_ready = sem("setup_done")
        s_xl = [sem("router_x_loaded0"), sem("router_x_loaded1")]
        s_rt = sem("router_logits")
        s_rc = sem("router_copied")
        s_gm = sem("gate_math")
        s_ge = sem("gate_exp")
        s_pad = sem("padding_stored")
        s_dt = sem("dt_broadcast")
        s_exp = sem("dA_ready")
        s_dtx = sem("dtx_broadcast")
        s_gr = sem("gate_rows")
        s_gated = sem("hidden_gated")
        s_mul = sem("dBx_ready")
        s_scan = sem("h_ready")
        s_hc = sem("hC_ready")
        s_carry = sem("carry_ready")
        s_y = sem("y_summed")
        s_ev = sem("y_evacuated")
        s_pr = [sem("work_bank0_ready"), sem("work_bank1_ready")]
        s_pf = [sem("work_bank0_free"), sem("work_bank1_free")]
        s_sp = [sem("softplus_steps0"), sem("softplus_steps1")]
        s_s = sem("dtx_ready")
        s_cast = sem("split_cast")
        s_r1 = sem("split_rest")
        s_lo = sem("split_low")
        s_pk = sem("packed")
        s_win = [sem("window0_loaded"), sem("window1_loaded")]
        s_wfree = sem("window_free")
        s_xp = sem("piece_loaded")
        s_sqr = sem("ln_square")
        s_rs = sem("ln_rstd")
        s_xn = sem("ln_done")
        s_x2s = sem("x2_stored")
        s_xns = sem("xn_stored")
        s_fin = sem("gated_y")
        s_xf = sem("residual_loaded")
        s_out = sem("out_stored")

        PKB = 16 * 24

        block = ctx.enter_context(nc.Block())


        def body_number(img, q, rev, odd):
            return img * BODIES + q * 2 + (NCH * rev + odd)

        def piece_number(img, q, rev):
            return NCH + img * NCH + q + (NCH // 2) * rev

        def next_image(img):
            return (img + 1) % IMGS

        @block.sync
        def _(sp):
            def wait_then_address(semaphore, value):
                sp.wait_ge(s_ld, 16 * N_LOADS)
                sp.wait_ge(semaphore, value)

            loads = [
                (w1[:, :], A["w1T"]), (w2[:, :, :], A["w2T"]), (b1[:, :], A["b1"]), (b2f[:, :], A["b2"]),
                (wr[:, :], A["wrT"]), (w_in[:, :], A["w_in"]), (gam[:, :], A["gamma"]), (bet[:, :], A["beta"]),
                (cb[0][:, :], A["conv_b"][0:P, :]), (cb[1][:, :], A["conv_b"][P:DI, :]),
                (wx[0][:, :], A["w_x"][0:P, :]), (wx[1][:, :], A["w_x"][P:DI, :]), (wxT[:, :], A["w_xT"]),
                (wdt[:, :], A["w_dt"]), (bd[0][:, :], A["b_dt"][0:P, :]), (bd[1][:, :], A["b_dt"][P:DI, :]),
                (amat[:, :], A["a_log"]), (dvec[0][:, :], A["d"][0:P, :]), (dvec[1][:, :], A["d"][P:DI, :]),
                (wo0[:, :], A["w_out"][0:P, :]), (wo1[:, :], A["w_out_low"]),
                (red[:, :, :], A["c_red"].rearrange("p (r c) -> p r c", r=4)), (ident[:, :], A["c_ident"]),
                (mean[:, :], A["c_mean"]),
                (hid[0:3 * GRP, 0, :], A["c_sel"]),
                (hid[0:3 * E, 1, :], A["c_gate"][:, 0:CH]), (hid[0:3 * E, 2, 0:HT * P - CH], A["c_gate"][:, CH:HT * P]),
                (scl[:, :], A["scale"].partition_broadcast(P)), (rb[:, :], A["router_b"].partition_broadcast(P)),
                (ys0[0:C + 1, 0:TAPS * DI], A["conv_w"].partition_broadcast(C + 1)),
            ]
            for credit in (s_x2s, s_xns, s_out):
                sp.sem_inc(credit, 16)
            for out, src in loads:
                sp.dma_start(out, src).then_inc(s_ld, 16)
            assert len(loads) == N_LOADS
            HALF = PIX // 2
            with sp.Fori(0, IMGS) as i:
                for half in range(2):
                    wait_then_address(s_rt, i * 2 + half + 1)
                    sp.dma_start(hc[0:C, 4 * half:4 * half + 4, :],
                                 A["x"][bass.ds(i, 1), :, half * HALF:(half + 1) * HALF].rearrange("o c (a t) -> (o c) a t", a=4)
                                 ).then_inc(s_xl[half], 16)
            sp.wait_ge(s_ready, 1)
            for i in range(IMGS):
                sp.dma_start(xn_d[i, :, 0:TAPS - 1], ys0[0:C + 1, 1024:1024 + TAPS - 1]).then_inc(s_pad, 16)
                sp.dma_start(xn_d[i, :, PADW - (TAPS - 1):PADW], ys0[0:C + 1, 1024:1024 + TAPS - 1]).then_inc(s_pad, 16)
                for k in range(PIX // 1024):
                    sp.dma_start(xn_d[i, C:C + 1, TAPS - 1 + 1024 * k:TAPS - 1 + 1024 * (k + 1)],
                                 ys0[0:1, 2048:3072]).then_inc(s_pad, 16)

            def load_piece(image, j, pc):
                wait_then_address(s_xn, pc + 1)
                sp.dma_start(xp[:, :], A["x"][bass.ds(image, 1), :, bass.ds(j * CH, CH)].rearrange("o c t -> (o c) t")).then_inc(s_xp, 16)

            def store_x2(image, j, pc, u):
                bank, at = u.at["Y2"]
                wait_then_address(s_pf[bank], at + 2)
                sp.dma_start(x2_d[bass.ds(image, 1), :, bass.ds(j * CH, CH)].rearrange("o c t -> (o c) t"), x2p[:, :]).then_inc(s_x2s, 16)

            def store_xn(image, j, pc):
                wait_then_address(s_xn, pc + 2)
                sp.dma_start(xn_d[bass.ds(image, 1), 0:C, bass.ds(TAPS - 1 + j * CH, CH)].rearrange("o c t -> (o c) t"), xnp[:, :]).then_inc(s_xns, 16)

            def load_window(image, chunk, par, pieces):
                if pieces is not None:
                    wait_then_address(s_xns, pieces * 16 + 16)
                sp.dma_start(win[:, par, :], xn_d[bass.ds(image, 1), :, bass.ds(chunk * CH, WIN)].rearrange("o c t -> (o c) t")).then_inc(s_win[par], 16)

            def pack(part, par):
                rows = slice(GRP * part, GRP * part + GRP)
                for g in range(4):
                    sp.dma_start(pk[rows, par, :, g, :], spl[GRP * g:GRP * g + GRP, part, 0:2, :]).then_inc(s_pk, 16)
                for k in range(4):
                    sp.dma_start(pk[rows, par, k // 2, 4 + k % 2, :], spl[GRP * k:GRP * k + GRP, part, 2, :]).then_inc(s_pk, 16)

            with sp.Fori(0, NCH) as j:
                load_piece(0, j, j)
                store_x2(0, j, j, piece_uses(j))
                store_xn(0, j, j)
            sp.wait_ge(s_pad, 16 * (2 + PIX // 1024) * IMGS)
            for c in range(2):
                load_window(0, c, c, NCH)
            sp.wait_ge(s_cast, 1)
            pack(0, 0)
            sp.wait_ge(s_cast, 2)
            pack(1, 0)
            sp.wait_ge(s_lo, 2)
            pack(2, 0)

            def store_out(img, chunk, at):
                wait_then_address(s_pf[1], at + 2)
                sp.dma_start(A["out"][bass.ds(img, 1), :, bass.ds(chunk * CH, CH)].rearrange("o c t -> (o c) t"), ob[:, :]).then_inc(s_out, 16)

            def load_residual(img, chunk, f):
                wait_then_address(s_x2s, (img + 1) * (NCH * 16) + 16)
                sp.dma_start(xf[:, :], x2_d[bass.ds(img, 1), :, bass.ds(chunk * CH, CH)].rearrange("o c t -> (o c) t")).then_inc(s_xf, 16)

            def body(img, q, rev, odd, last, fin, u):
                n, pc = body_number(img, q, rev, odd), piece_number(img, q, rev)
                par, j = odd, q + (NCH // 2) * rev
                nimg = next_image(img)
                sp.wait_ge(s_dt, n * NT + LEAD_DT)
                sp.sem_inc(s_wfree, 1)
                if last and rev:
                    pass
                elif last:
                    load_window(img, NCH - 1 - odd, par, None)
                else:
                    load_window(img, chunk_of(q, rev, odd) + (-2 if rev else 2), par, None if rev else (img + 1) * NCH)
                if not odd:
                    load_piece(nimg, j, pc)
                if fin:
                    load_residual(img, chunk_of(q, rev, odd) + 1, None)
                if last and rev:
                    sp.wait_ge(s_xns, ((img + 1) * NCH + (NCH // 2)) * 16 + 16)
                sp.wait_ge(s_cast, 2 * n + 3)
                pack(0, 1 - par)
                if last and rev:
                    load_window(nimg, odd, par, None)
                if fin:
                    store_out(img, chunk_of(q, rev, odd) + 1, u.at["OUT"][1])
                sp.wait_ge(s_cast, 2 * n + 4)
                pack(1, 1 - par)
                sp.wait_ge(s_lo, n + 3)
                pack(2, 1 - par)
                if odd:
                    store_x2(nimg, j, pc, u)
                    store_xn(nimg, j, pc)

            def tail(img, u):
                load_residual(img, 0, None)
                store_out(img, 0, u.at["OUT"][1])

            bodies(sp, body, tail)
            sp.wait_ge(s_out, 16 * IMGS * NCH + 16)
            sp.wait_ge(s_x2s, 16 * NCH * (IMGS + 1) + 16)
            sp.wait_ge(s_xns, 16 * NCH * (IMGS + 1) + 16)
            for k in range(2):
                sp.wait_ge(s_win[k], 16 * (IMGS * BODIES // 2 + 1))
            sp.wait_ge(s_pk, PKB * (IMGS * BODIES + 1))

        @block.tensor
        def _(pe):
            mm = nc.tensor.matmul
            pe.wait_ge(s_ld, 16 * N_LOADS)
            mm(ps[0][0:1, 0:DI + 2 * P], bet[:, :], w_in[:, :], start=True, stop=True).then_inc(s_setup_pe, 1)
            mm(ps[1][:, 0:DI], wxT[:, 0:P], wdt[:, :], start=True, stop=True).then_inc(s_setup_pe, 1)
            mm(ps[2][0:DR, 0:DI], wxT[:, P:DI], wdt[:, :], start=True, stop=True).then_inc(s_setup_pe, 1)
            pe.sem_inc(s_rt, 2)
            with pe.Fori(0, IMGS) as i:
                for half in range(2):
                    pe.wait_ge(s_xl[half], i * 16 + 16)
                    pe.wait_ge(s_rc, i * 2 + half + 1)
                    for b in range(16):
                        last = mm(ps[6 + half][:, E * b:E * b + E], hc[0:C, 4 * half + b // 4, P * (b % 4):P * (b % 4) + P],
                                  wr[:, :], start=True, stop=True)
                    last.then_inc(s_rt, 1)

            def begin(u, name):
                bank, at = u.at[name]
                pe.wait_ge(s_pf[bank], at + 1)
                return p_w[bank]

            def ready(u, name, last):
                last.then_inc(s_pr[u.at[name][0]], 1)

            def gates_transposed(image, j, u):
                out = begin(u, "GT")
                for s in range(4):
                    last = mm(out[0:3 * E, P * s:P * s + P],
                              g3[:, bass.ds(image * (PIX // P) + (j * 4 + s), 1), :].rearrange("p o e -> p (o e)"),
                              identb[:, :], start=True, stop=True)
                ready(u, "GT", last)

            def hidden(m, pc, u):
                if m == 0:
                    pe.wait_ge(s_xp, pc * 16 + 16)
                ready(u, f"H{m}", mm(begin(u, f"H{m}")[:, :], w1[:, P * m:P * m + P], xp[:, :], start=True, stop=True))

            def gate_rows(m, pc, bank, gt):
                pe.wait_ge(s_pf[1], gt.at["GT"][1] + 2)
                mm(p_ring[bank][:, :], gsel[:, m, :], gT[:, :], start=True, stop=True).then_inc(s_gr, 1)

            def expert_out(m, u, pc):
                if m == 0:
                    begin(u, "Y2")
                pe.wait_ge(s_gated, pc * HT + (m + 1 + RING))
                mm(p_w[1][0:C, :], w2[:, m, :], hid[:, m, :], start=(m == 0), stop=False)

            def expert_bias(u):
                for s in range(3):
                    last = mm(p_w[1][0:C, :], b2s[:, s, :], gT[:, :], start=False, stop=(s == 2))
                ready(u, "Y2", last)

            def ln_mean(u):
                pe.wait_ge(s_pf[1], u.at["Y2"][1] + 2)
                ready(u, "MU", mm(begin(u, "MU")[0:C, :], mean[:, :], x2p[:, :], start=True, stop=True))

            def ln_var(pc, u):
                pe.wait_ge(s_sqr, pc + 1)
                ready(u, "VAR", mm(begin(u, "VAR")[0:C, :], mean[:, :], sq[:, :], start=True, stop=True))

            def project(half, first, k, par, rev, u):
                name, lo, m = f"U{half}", P * half, (P, DR)[half]
                if first:
                    begin(u, name)
                for t in (k, k + 1):
                    at = 2 * (TAPS - 1) - t if rev else t
                    last = mm(p_w[half][0:m, :], w_u[:, t, lo:lo + m], win[:, par, at:at + CH],
                              start=(t == 0), stop=(t == TAPS - 1))
                if not first:
                    ready(u, name, last)

            def project_z(half, par, u):
                lo = DI + P * half
                ready(u, f"Z{half}", mm(begin(u, f"Z{half}")[:, :], w_g[:, lo:lo + P], win[:, par, TAPS - 1:TAPS - 1 + CH],
                                        start=True, stop=True))

            def from_xr(name, w0, w1_, par, u):
                out = begin(u, name)
                mm(out[:, :], w0, xr[0][:, par, :], start=True, stop=False)
                ready(u, name, mm(out[:, :], w1_, xr[1][:, par, :], start=False, stop=True))

            def project_dt(half, par, u):
                lo = P * half
                from_xr(f"D{half}", w_d[0][:, lo:lo + P], w_d[1][:, lo:lo + P], par, u)

            def project_c(par, u):
                from_xr("C", w_c[0][:, :], w_c[1][:, :], par, u)

            def bc(which, dst, i, par):
                ch, r, _, _ = TILES[i]
                return mm(dst[:, :], sel[:, r, :], pk[:, par, which, ch // GRP, :], start=True, stop=True)

            def bc_dt(n, i, par):
                if i == 0:
                    pe.wait_ge(s_pk, (n + 1) * PKB)
                pe.wait_ge(s_exp, n * NT + (i + 1))
                bc(0, p_dt[i % 2], i, par).then_inc(s_dt, 1)

            def through_ring(n, pc, odd, upto, gt):
                elements = ring(odd)
                k1 = elements.index(("tile", upto))
                k0 = elements.index(("tile", upto - 1)) + 1 if upto else 0
                for k in range(k0, k1 + 1):
                    was, at = elements[k - RING] if k >= RING else ("tile", NT - RING + k - NT)
                    if was == "tile":
                        pe.wait_ge(s_scan, n * NT + (at + 1 + 8))
                    else:
                        pe.wait_ge(s_gated, pc * HT + (at + 1 + RING))
                    kind, at = elements[k]
                    if kind == "tile":
                        bc(1, p_ring[k % RING], at, odd).then_inc(s_dtx, 1)
                    else:
                        gate_rows(at, pc, k % RING, gt)

            def d_times_x(n, low, par):
                pe.wait_ge(s_ev, n * 2 + (2 if low else 3))
                k = 1 if low else 0
                mm(p_y[:, :], diag[k][:, :], xr[k][:, par, :], start=True, stop=False, skip_group_check=True)

            def sum_states(n, r):
                pe.wait_ge(s_hc, n * NT + (BATCH * (r + 1) + 8))
                for i in range(BATCH * r, BATCH * r + BATCH):
                    _, _, row, col = TILES[i]
                    last = mm(p_y[GRP * col:GRP * col + GRP, :], red[:, row, :], hc[:, i % NH, :], start=False,
                              stop=(r in (LOW_BATCHES - 1, NB - 1)), skip_group_check=True)
                last.then_inc(s_y, 1)

            def finish(u, f):
                pe.wait_ge(s_fin, f * 4 + 4)
                out = begin(u, "OUT")
                mm(out[0:C, :], wo0[:, :], yr0[:, :], start=True, stop=False)
                ready(u, "OUT", mm(out[0:C, :], wo1[:, :], yr1[:, :], start=False, stop=True))

            pe.wait_ge(s_ready, 1)
            with pe.Fori(0, NCH) as j:
                u = piece_uses(j)
                gates_transposed(0, j, u)
                for m in range(HT):
                    hidden(m, j, u)
                for m in range(HT):
                    pe.wait_ge(s_gated, j * HT + (m + 1))
                    gate_rows(m, j, m % RING, u)
                for m in range(HT):
                    expert_out(m, u, j)
                expert_bias(u)
                ln_mean(u)
                ln_var(j, u)
            first, second, rest = prologue_uses()
            for par, u in ((0, first), (1, second)):
                pe.wait_ge(s_win[par], 16)
                for half in range(2):
                    project(half, True, 0, par, 0, u)
                    project(half, False, 2, par, 0, u)
            for k in range(2):
                bank, at = second.at[f"U{k}"]
                pe.wait_ge(s_pf[bank], at + 2)
            project_dt(0, 0, rest)
            project_dt(1, 0, rest)
            project_c(0, rest)
            for i in range(LEAD_DT):
                bc_dt(0, i, 0)
            for i in range(LEAD_DTX):
                through_ring(0, 0, 0, i, None)

            even = [None]

            def body(img, q, rev, odd, last, fin, u):
                n, pc = body_number(img, q, rev, odd), piece_number(img, q, rev)
                par, nxt, j = odd, 1 - odd, q + (NCH // 2) * rev
                nrev = (rev == 1) != (last and odd == 1)
                urev = (rev == 1) != last
                nimg = next_image(img)
                gt = even[0] if odd else u
                if not odd:
                    even[0] = u

                def taps(half, first):
                    project(half, first, 0 if first else 2, par, urev, u)

                for i in range(NT):
                    if i + LEAD_DT < NT:
                        bc_dt(n, i + LEAD_DT, par)
                    else:
                        bc_dt(n + 1, i + LEAD_DT - NT, nxt)
                    if i + LEAD_DTX < NT:
                        through_ring(n, pc, odd, i + LEAD_DTX, gt)
                    else:
                        through_ring(n + 1, pc, nxt, i + LEAD_DTX - NT, gt)
                    if i == 0:
                        project_dt(0, nxt, u)
                    if i == 2:
                        project_dt(1, nxt, u)
                    if i == 6:
                        project_c(nxt, u)
                    if i == 7 and fin:
                        finish(u, img * NCH + q * 2 + odd - 1)
                    if i == (11 if odd else 12):
                        pe.wait_ge(s_win[par], (img * (BODIES // 2) + q + ((NCH // 2) * rev + 2)) * 16)
                    if not odd:
                        if i == 0:
                            gates_transposed(nimg, j, u)
                        if i == 9:
                            hidden(0, pc, u)
                            hidden(1, pc, u)
                        if i == 11:
                            hidden(2, pc, u)
                        if i in (12, 13, 14, 15):
                            taps((i - 12) // 2, i % 2 == 0)
                        if i == 17 and nrev:
                            project_z(0, nxt, u)
                        if i == 18:
                            hidden(3, pc, u)
                        if i == 20:
                            hidden(4, pc, u)
                        if i == 22:
                            hidden(5, pc, u)
                            if nrev:
                                project_z(1, nxt, u)
                    else:
                        if i in (8, 9, 10):
                            expert_out(2 * (i - 8), u, pc)
                            expert_out(2 * (i - 8) + 1, u, pc)
                        if i == 11:
                            expert_bias(u)
                        if i in (11, 12):
                            taps(0, i == 11)
                        if i == 13:
                            ln_mean(u)
                        if i in (15, 16):
                            taps(1, i == 15)
                        if i == 18:
                            ln_var(pc, u)
                        if i == 19 and nrev:
                            project_z(0, nxt, u)
                        if i == 22 and nrev:
                            project_z(1, nxt, u)
                    if i == 5:
                        d_times_x(n, True, par)
                    if i == 13:
                        d_times_x(n, False, par)
                    if i % BATCH == 2 and i >= 6:
                        sum_states(n, (i - 6) // BATCH)
                sum_states(n, NB - 1)

            def tail(img, u):
                finish(u, img * NCH + (NCH - 1))

            bodies(pe, body, tail)

        @block.scalar
        def _(act):
            A_ = nc.scalar.activation
            act.sem_inc(s_exp, 2)
            act.sem_inc(s_ev, 2)
            act.sem_inc(s_pf[0], 1)
            act.sem_inc(s_pf[1], 1)
            act.wait_ge(s_setup_pe, 3)
            A_(w_g[C:C + 1, :], ps[0][0:1, 0:DI + 2 * P], ACT.Copy).then_inc(s_setup_act, 1)
            A_(w_d[0][:, 0:DI], ps[1][:, 0:DI], ACT.Copy).then_inc(s_setup_act, 1)
            A_(w_d[1][:, 0:DI], ps[2][0:DR, 0:DI], ACT.Copy).then_inc(s_setup_act, 1)
            A_(amat[:, :], amat[:, :], ACT.Exp).then_inc(s_setup_act, 1)
            act.wait_ge(s_gm, 1)
            A_(dA[:, 0:2, :], dA[:, 0:2, :], ACT.Exp).then_inc(s_ge, 1)
            act.wait_ge(s_ready, 1)

            def begin(u, name):
                bank, at = u.at[name]
                act.wait_ge(s_pr[bank], at + 1)
                return p_w[bank]

            def free(u, name, ins):
                ins.then_inc(s_pf[u.at[name][0]], 1)

            def main_tables():
                nc.scalar.preload_act_table_set("natural_log_exp_and_others")

            def copy_gates(u):
                free(u, "GT", A_(gT[:, :], begin(u, "GT")[0:3 * E, :], ACT.Copy))

            def gelu(ms, u):
                for m in ms:
                    free(u, f"H{m}", A_(hid[:, m, :], begin(u, f"H{m}")[:, :], ACT.Gelu, bias=b1[:, m:m + 1]))
                main_tables()

            def ln_square(u, pc):
                act.wait_ge(s_pf[1], u.at["MU"][1] + 2)
                A_(sq[:, :], xc[:, :], ACT.Square).then_inc(s_sqr, 1)

            def ln_rstd(u, pc):
                out = begin(u, "VAR")
                free(u, "VAR", A_(sq[:, :], out[0:C, :], ACT.Ln, bias=EPS[0:C, :]))
                act.wait_ge(s_pf[0], u.at["VAR"][1] + 2)
                A_(sq[:, :], sq[:, :], ACT.Exp, scale=-0.5).then_inc(s_rs, 1)

            def silu_x(u, par):
                for k, m in enumerate((P, DR)):
                    free(u, f"U{k}", A_(xr[k][:, par, :], begin(u, f"U{k}")[0:m, :], ACT.Silu, bias=cb[k][:, :]))

            def silu_z(n, cpar):
                act.wait_ge(s_exp, n * NT + (LEAD_DT + 1 + 2))
                A_(sz0[:, cpar, :], sz0[:, cpar, :], ACT.Silu)
                A_(sz1[:, cpar, :], sz1[:, cpar, :], ACT.Silu)

            def copy_z(half, u, cpar, f):
                out = begin(u, f"Z{half}")
                if f is not None and half == 0:
                    act.wait_ge(s_fin, f * 4 + 4)
                free(u, f"Z{half}", A_((sz1 if half else sz0)[:, cpar, :], out[:, :], ACT.Copy))

            V_OF = (S[:, 0, :], S[0:DR, 2, :])
            ROWS_OF = (P, DR)

            def sp_relu(k, u, b):
                if k == 0:
                    act.wait_ge(s_lo, b + 1)
                m = ROWS_OF[k]
                A_(V_OF[k], begin(u, f"D{k}")[0:m, :], ACT.Relu, bias=nbd[k][:, :], scale=-1.0).then_inc(s_sp[k], 1)

            def sp_exp(k, b):
                act.wait_ge(s_sp[k], b * 3 + 1)
                A_(V_OF[k], V_OF[k], ACT.Exp, bias=SPM[0:ROWS_OF[k], :], scale=-1.0).then_inc(s_sp[k], 1)

            def sp_log(k, b):
                act.wait_ge(s_sp[k], b * 3 + 2)
                A_(V_OF[k], V_OF[k], ACT.Ln, bias=1.0).then_inc(s_sp[k], 1)

            def copy_b(half, u, par):
                if half == 0:
                    begin(u, "D1")
                A_(bB[DR * half:DR * half + DR, par, :], p_w[u.at["D1"][0]][DR:P, :], ACT.Copy)

            def copy_c(u, par):
                free(u, "C", A_(cC[:, par, :], begin(u, "C")[:, :], ACT.Copy))

            def cast_high(b):
                act.wait_ge(s_s, b * 2 + 2)
                if not isinstance(b, int):
                    act.wait_ge(s_pk, b * PKB)
                A_(spl[:, 0, :, :], S[:, :, :], ACT.Copy).then_inc(s_cast, 1)

            def cast_mid(b):
                act.wait_ge(s_r1, b + 2)
                A_(spl[:, 1, :, :], S[:, :, :], ACT.Copy).then_inc(s_cast, 1)

            def exp_dA(n, i):
                act.wait_ge(s_dt, n * NT + (i + 1))
                act.wait_ge(s_scan, n * NT + (i - NA + 1 + 8))
                col = TILES[i][0] // CPT
                A_(dA[:, i % NA, :], p_dt[i % 2][:, :], ACT.Exp, scale=amat[:, col:col + 1]).then_inc(s_exp, 1)

            def evacuate(n, low, rev, chunk, u, fin):
                act.wait_ge(s_y, n * NB + (2 + (LOW_BATCHES if low else NB)))
                if fin:
                    act.wait_ge(s_pf[1], u.at["OUT"][1] + 2)
                if rev:
                    dst = (yr1 if low else yr0)[:, :]
                else:
                    dst = (ys1 if low else ys0)[:, bass.ds(chunk * CH, CH)]
                A_(dst, p_y[:, :], ACT.Copy).then_inc(s_ev, 1)

            with act.Fori(0, NCH) as j:
                u = piece_uses(j)
                copy_gates(u)
                gelu(range(HT), u)
                ln_square(u, j)
                ln_rstd(u, j)
            first, second, rest = prologue_uses()
            silu_x(first, 0)
            silu_x(second, 1)
            main_tables()
            for k in range(2):
                sp_relu(k, rest, 0)
                sp_exp(k, 0)
                if k == 1:
                    copy_b(0, rest, 0)
                    copy_b(1, rest, 0)
                sp_log(k, 0)
            copy_c(rest, 0)
            cast_high(0)
            cast_mid(0)
            for i in range(LEAD_DT):
                exp_dA(0, i)

            def body(img, q, rev, odd, last, fin, u):
                n, pc = body_number(img, q, rev, odd), piece_number(img, q, rev)
                nxt = 1 - odd
                nrev = (rev == 1) != (last and odd == 1)
                f = img * NCH + q * 2 + odd - 1 if fin else None
                z_at = (20, 22) if odd else (19, 23)
                for i in range(NT):
                    exp_dA(*((n, i + LEAD_DT) if i + LEAD_DT < NT else (n + 1, i + LEAD_DT - NT)))
                    if i == 1:
                        sp_relu(0, u, n + 1)
                    if i == 2:
                        sp_exp(0, n + 1)
                    if i == 3:
                        sp_relu(1, u, n + 1)
                        copy_b(0, u, nxt)
                    if i == 4:
                        sp_log(0, n + 1)
                        sp_exp(1, n + 1)
                    if i == 5:
                        copy_b(1, u, nxt)
                        sp_log(1, n + 1)
                    if i == 8:
                        cast_high(n + 1)
                        copy_c(u, nxt)
                    if i == 12:
                        evacuate(n, True, rev, q * 2 + odd, u, fin)
                    if i == 13:
                        cast_mid(n + 1)
                    if i == (17 if odd else 16):
                        silu_x(u, odd)
                        if rev:
                            silu_z(n, 1 - odd)
                        main_tables()
                    if nrev and i in z_at:
                        copy_z(z_at.index(i), u, 1 - nxt, f)
                    if not odd:
                        if i == 1:
                            copy_gates(u)
                        if i == 10:
                            gelu((0, 1, 2), u)
                        if i == 21:
                            gelu((3, 4, 5), u)
                    else:
                        if i == 15:
                            ln_square(u, pc)
                        if i == 20:
                            ln_rstd(u, pc)
                evacuate(n, False, rev, q * 2 + odd, u, fin)

            def tail(img, u):
                pass

            bodies(act, body, tail)

        @block.vector
        def _(dve):
            V = nc.vector
            dve.sem_inc(s_scan, 8)
            dve.sem_inc(s_rc, 2)
            dve.sem_inc(s_gated, RING)
            step = [0]

            def link(ins):
                step[0] += 1
                ins.then_inc(s_cst, 1)
                dve.wait_ge(s_cst, step[0])

            dve.wait_ge(s_ld, 16 * N_LOADS)
            link(V.memset(konst[:, 0:1], LN_EPS))
            link(V.memset(konst[:, 1:2], SP_MAX))
            link(V.tensor_copy(sel[:, :, :], hid[0:3 * GRP, 0, :].rearrange("p (r c) -> p r c", r=4)))
            link(V.tensor_copy(gsel[:, 0:4, :], hid[0:3 * E, 1, :].rearrange("p (r c) -> p r c", r=4)))
            link(V.tensor_copy(gsel[:, 4:6, :], hid[0:3 * E, 2, 0:2 * P].rearrange("p (r c) -> p r c", r=2)))
            link(V.tensor_copy(identb[:, :], ident[:, :]))
            link(V.tensor_scalar(w2[:, :, :], w2[:, :, :], scl[:, :], None, ALU.mult))
            link(V.tensor_scalar(b2f[:, :], b2f[:, :], scl[0:3 * E, :], None, ALU.mult))
            link(V.tensor_copy(b2s[:, 0, :], b2f[:, :]))
            link(V.tensor_tensor(b2r[:, :], b2f[:, :], b2s[:, 0, :], ALU.subtract))
            link(V.tensor_copy(b2s[:, 1, :], b2r[:, :]))
            link(V.tensor_tensor(b2s[:, 2, :], b2r[:, :], b2s[:, 1, :], ALU.subtract))
            link(V.tensor_scalar(w_g[0:C, :], w_in[:, :], gam[:, :], None, ALU.mult))
            link(V.tensor_scalar(wo0[:, :], wo0[:, :], 0.5, None, ALU.mult))
            link(V.tensor_scalar(wo1[:, :], wo1[:, :], 0.5, None, ALU.mult))
            for k in range(2):
                m = (P, DR)[k]
                link(V.tensor_scalar(nbd[k][:, :], bd[k][:, :], -1.0, SP_MAX, ALU.mult, ALU.add))
                if k == 0:
                    out, eye = diag[k][:, :], ident[:, :]
                else:
                    link(V.memset(diag[k][:, :], 0.0))
                    out = diag[k][:, :].rearrange("p (j c) -> p j c", j=4)[:, :, 0:QUART]
                    eye = ident[0:m, 0:m].rearrange("p (j c) -> p j c", j=4)
                link(V.tensor_scalar(out, eye, dvec[k][:, :], None, ALU.mult))
                for w, lo, c in ((w_d[k][:, DI:2 * P], RANK, CPT // 2), (w_c[k][:, :], RANK + NST, CPT)):
                    link(V.tensor_copy(w.rearrange("p (c s) -> p c s", c=c),
                                       wx[k][:, lo:lo + NST].unsqueeze(1).to_broadcast([m, c, NST])))
            dve.wait_ge(s_setup_act, 4)
            link(V.tensor_scalar(amat[:, :], amat[:, :], -1.0, None, ALU.mult))
            cw = ys0[0:C + 1, 0:TAPS * DI].rearrange("p (k c) -> p k c", k=TAPS)
            for k in range(TAPS):
                link(V.tensor_tensor(w_u[:, k, :], w_g[:, 0:DI], cw[:, k, :], ALU.mult))
            link(V.memset(ys0[0:C + 1, 1024:1024 + TAPS - 1], 0.0))
            link(V.memset(ys0[0:1, 2048:3072], 1.0))

            lg = dA[:, 2:4, :].rearrange("p a t -> p (a t)").rearrange("p (b e) -> p b e", e=E)
            with dve.Fori(0, IMGS) as i:
                for half in range(2):
                    dve.wait_ge(s_rt, i * 2 + half + 3)
                    V.tensor_tensor(lg[:, bass.ds(i * 32 + 16 * half, 16), :],
                                    ps[6 + half][:, 0:16 * E].rearrange("p (b e) -> p b e", e=E),
                                    rb[:, :].unsqueeze(1).to_broadcast([P, 16, E]), ALU.add).then_inc(s_rc, 1)
            dve.wait_ge(s_rc, 2 + 2 * IMGS)

            def tmp(a, b):
                return h[:, a:b, :].rearrange("p a t -> p (a t)").rearrange("p (b e) -> p b e", e=E)

            rank, cmp_, gate = tmp(0, 2), tmp(2, 4), tmp(4, 6)
            eg = dA[:, 0:2, :].rearrange("p a t -> p (a t)").rearrange("p (b e) -> p b e", e=E)
            mx = h[:, 6, 0:BLK]
            link(V.memset(rank, 0.0))
            for j in range(E):
                lj = lg[:, :, j:j + 1]
                if j > 0:
                    link(V.tensor_tensor(cmp_[:, :, 0:j], lj.to_broadcast([P, BLK, j]), lg[:, :, 0:j], ALU.is_gt))
                    link(V.tensor_tensor(rank[:, :, 0:j], rank[:, :, 0:j], cmp_[:, :, 0:j], ALU.add))
                if j < E - 1:
                    k = E - 1 - j
                    link(V.tensor_tensor(cmp_[:, :, j + 1:E], lj.to_broadcast([P, BLK, k]), lg[:, :, j + 1:E], ALU.is_ge))
                    link(V.tensor_tensor(rank[:, :, j + 1:E], rank[:, :, j + 1:E], cmp_[:, :, j + 1:E], ALU.add))
            link(V.tensor_scalar(rank, rank, 1.5, None, ALU.is_lt))
            link(V.reduce_max(mx, lg, AX.X))
            V.tensor_tensor(eg, lg, mx.unsqueeze(2).to_broadcast([P, BLK, E]), ALU.subtract).then_inc(s_gm, 1)
            dve.wait_ge(s_ge, 1)
            link(V.tensor_tensor(gate, eg, rank, ALU.mult))
            link(V.reduce_sum(mx, gate, AX.X))
            link(V.reciprocal(mx, mx))
            link(V.tensor_tensor(gate, gate, mx.unsqueeze(2).to_broadcast([P, BLK, E]), ALU.mult))
            link(V.tensor_copy(g3[:, :, 0:E], gate))
            link(V.tensor_tensor(gate, gate, g3[:, :, 0:E], ALU.subtract))
            link(V.tensor_copy(g3[:, :, E:2 * E], gate))
            link(V.tensor_tensor(g3[:, :, 2 * E:3 * E], gate, g3[:, :, E:2 * E], ALU.subtract))
            dve.sem_inc(s_ready, 1)

            def begin(u, name):
                bank, at = u.at[name]
                dve.wait_ge(s_pr[bank], at + 1)
                return p_w[bank]

            def free(u, name, ins):
                ins.then_inc(s_pf[u.at[name][0]], 1)

            def gate_hidden(m, pc, bank, u):
                dve.wait_ge(s_gr, pc * HT + (m + 1))
                of, at = u.at[f"H{m}"]
                dve.wait_ge(s_pf[of], at + 2)
                V.tensor_tensor(hid[:, m, :], p_ring[bank][:, :], hid[:, m, :], ALU.mult).then_inc(s_gated, 1)

            def residual(u, pc):
                out = begin(u, "Y2")
                dve.wait_ge(s_xp, pc * 16 + 16)
                dve.wait_ge(s_x2s, pc * 16 + 16)
                free(u, "Y2", V.tensor_tensor(x2p[:, :], out[0:C, :], xp[:, :], ALU.add))

            def centre(u):
                out = begin(u, "MU")
                dve.wait_ge(s_pf[1], u.at["Y2"][1] + 2)
                free(u, "MU", V.scalar_tensor_tensor(xc[:, :], out[0:C, :], -1.0, x2p[:, :], op0=ALU.mult, op1=ALU.add))

            def dt_max(k, u, b):
                m = (P, DR)[k]
                out = begin(u, f"D{k}")
                dve.wait_ge(s_sp[k], b * 3 + 3)
                v = (S[:, 0, :], S[0:DR, 2, :])[k]
                free(u, f"D{k}", V.scalar_tensor_tensor(v, out[0:m, :], bd[k][:, :], v, op0=ALU.add, op1=ALU.max))

            def dt_x(k, u, par):
                bank, at = u.at[f"D{k}"]
                dve.wait_ge(s_pf[bank], at + 2)
                out, v = ((S[:, 1, :], S[:, 0, :]), (S[DR:P, 2, :], S[0:DR, 2, :]))[k]
                V.tensor_tensor(out, v, xr[k][:, par, :], ALU.mult).then_inc(s_s, 1)

            def times_b(n, i, odd):
                if i == 0:
                    dve.wait_ge(s_cast, n * 2 + 2)
                dve.wait_ge(s_dtx, n * NT + (i + 1))
                bank = p_ring[ring(odd).index(("tile", i)) % RING]
                V.tensor_tensor(bank[:, :], bank[:, :], bB[:, odd, :], ALU.mult).then_inc(s_mul, 1)

            def scan(n, i, rev, odd):
                if i % BATCH == 0:
                    dve.wait_ge(s_carry, n * NB + (i // BATCH + 5))
                dve.wait_ge(s_exp, n * NT + (i + 1 + 2))
                dve.wait_ge(s_hc, n * NT + (i - NH + 1 + 8))
                dve.wait_ge(s_mul, n * NT + (i + 1))
                bank = p_ring[ring(odd).index(("tile", i)) % RING]
                a, b, o = dA[:, i % NA, :], bank[:, :], h[:, i % NH, :]
                if rev:
                    a, b, o = a[:, ::-1], b[:, ::-1], o[:, ::-1]
                V.tensor_tensor_scan(o, a, b, carry[:, i:i + 1], ALU.mult, ALU.add).then_inc(s_scan, 1)

            def add_residual(u, f):
                out = begin(u, "OUT")
                dve.wait_ge(s_xf, f * 16 + 16)
                dve.wait_ge(s_out, f * 16 + 16)
                free(u, "OUT", V.tensor_tensor(ob[:, :], out[0:C, :], xf[:, :], ALU.add))

            with dve.Fori(0, NCH) as j:
                u = piece_uses(j)
                for m in range(HT):
                    gate_hidden(m, j, m % RING, u)
                residual(u, j)
                centre(u)
            _, _, rest = prologue_uses()
            for k in range(2):
                dt_max(k, rest, 0)
            for k in range(2):
                dt_x(k, rest, 0)
            times_b(0, 0, 0)

            even = [None]

            def body(img, q, rev, odd, last, fin, u):
                n, pc = body_number(img, q, rev, odd), piece_number(img, q, rev)
                nxt = 1 - odd
                made = even[0] if odd else u
                if not odd:
                    even[0] = u
                for i in range(NT):
                    if i == 5:
                        dt_max(0, u, n + 1)
                    if i == 6:
                        dt_max(1, u, n + 1)
                        dt_x(0, u, nxt)
                    if i == 7:
                        dt_x(1, u, nxt)
                    if i == 8 and fin:
                        add_residual(u, img * NCH + q * 2 + odd - 1)
                    if odd:
                        if i == 12:
                            residual(u, pc)
                        if i == 14:
                            centre(u)
                    for slot, m in GATES[odd]:
                        if slot == i:
                            gate_hidden(m, pc, ring(odd).index(("gate", m)) % RING, made)
                    if i + 1 < NT:
                        times_b(n, i + 1, odd)
                    else:
                        times_b(n + 1, 0, nxt)
                    scan(n, i, rev, odd)

            def tail(img, u):
                add_residual(u, img * NCH + (NCH - 1))

            bodies(dve, body, tail)

        @block.gpsimd
        def _(pool):
            G = nc.gpsimd
            pool.sem_inc(s_hc, 8)
            pool.sem_inc(s_r1, 1)
            pool.sem_inc(s_lo, 1)
            pool.sem_inc(s_xn, 1)
            pool.sem_inc(s_y, 2)
            pool.sem_inc(s_carry, NB - 1)
            G.memset(carry[:, :], 0.0).then_inc(s_carry, 1)

            def normalise(pc):
                pool.wait_ge(s_rs, pc + 1)
                pool.wait_ge(s_xns, pc * 16 + 16)
                G.tensor_tensor(xnp[:, :], xc[:, :], sq[:, :], ALU.mult).then_inc(s_xn, 1)

            def split_rest(b):
                pool.wait_ge(s_cast, b * 2 + 1)
                G.tensor_tensor(S[:, :, :], S[:, :, :], spl[:, 0, :, :], ALU.subtract).then_inc(s_r1, 1)

            def split_low(b):
                pool.wait_ge(s_cast, b * 2 + 2)
                G.tensor_tensor(spl[:, 2, :, :], S[:, :, :], spl[:, 1, :, :], ALU.subtract).then_inc(s_lo, 1)

            def gate_y(f, par, chunk):
                G.tensor_tensor(yr0[:, :], yr0[:, :], ys0[:, bass.ds(chunk * CH, CH)], ALU.add).then_inc(s_fin, 1)
                G.tensor_tensor(yr1[:, :], yr1[:, :], ys1[:, bass.ds(chunk * CH, CH)], ALU.add).then_inc(s_fin, 1)
                pool.wait_ge(s_fin, f * 4 + 1)
                G.tensor_tensor(yr0[:, :], yr0[:, :], sz0[:, par, :], ALU.mult).then_inc(s_fin, 1)
                pool.wait_ge(s_fin, f * 4 + 2)
                G.tensor_tensor(yr1[:, :], yr1[:, :], sz1[:, par, :], ALU.mult).then_inc(s_fin, 1)

            def times_c(n, i, par, reset):
                if i == 0:
                    pool.wait_ge(s_cast, n * 2 + 2)
                pool.wait_ge(s_scan, n * NT + (i + 1 + 8))
                if i % BATCH == 0:
                    pool.wait_ge(s_y, n * NB + (i // BATCH + 1))
                G.tensor_tensor(hc[:, i % NH, :], h[:, i % NH, :], cC[:, par, :], ALU.mult).then_inc(s_hc, 1)
                if i % BATCH == BATCH - 1:
                    cols = carry[:, i - BATCH + 1:i + 1]
                    if reset is None:
                        G.memset(cols, 0.0).then_inc(s_carry, 1)
                    else:
                        s0 = (i - BATCH + 1) % NH
                        G.tensor_copy(cols, h[:, s0:s0 + BATCH, reset]).then_inc(s_carry, 1)

            with pool.Fori(0, NCH) as j:
                normalise(j)
            split_rest(0)
            split_low(0)

            def body(img, q, rev, odd, last, fin, u):
                n, pc = body_number(img, q, rev, odd), piece_number(img, q, rev)
                par = odd
                reset = None if last and odd else (0 if rev else CH - 1)
                for i in range(NT):
                    if i == 1 and fin:
                        pool.wait_ge(s_ready, 1)
                        pool.wait_ge(s_ev, n * 2 + 2)
                        gate_y(img * NCH + q * 2 + odd - 1, odd, chunk_of(q, rev, odd) + 1)
                    if i == 9:
                        split_rest(n + 1)
                    if i == 13:
                        split_low(n + 1)
                    if i == 21 and odd:
                        normalise(pc)
                    times_c(n, i, par, reset)

            def tail(img, u):
                pool.wait_ge(s_ready, 1)
                pool.wait_ge(s_ev, (img + 1) * (BODIES * 2) + 2)
                gate_y(img * NCH + (NCH - 1), 0, 0)

            bodies(pool, body, tail)


N_LOADS = 30


def low_layout(rows, end):
    low = np.zeros((P, rows.shape[1]), rows.dtype)
    for j in range(4):
        low[GRP * j:GRP * j + QUART] = rows[end - DR + QUART * j:end - DR + QUART * (j + 1)]
    return np.concatenate([rows[:end - DR], low])


def kernel(**inputs):
    import concourse.bacc as _bacc
    from concourse.bass_utils import run_bass_kernel_spmd as _run

    a = {k: np.asarray(v) for k, v in inputs.items()}
    L0, L1 = "L0_conv_", "L1_conv_"
    laid = {
        "x": a["x"].reshape(IMGS, C, PIX),
        "w1T": a[L0 + "fc1_w"].transpose(2, 0, 1).reshape(C, E * HID),
        "w2T": a[L0 + "fc2_w"].transpose(0, 2, 1).reshape(HT, P, C).transpose(1, 0, 2),
        "b1": a[L0 + "fc1_b"].reshape(HT, P).T,
        "b2": np.tile(a[L0 + "fc2_b"], (3, 1)),
        "wrT": a[L0 + "router_w"].T,
        "router_b": a[L0 + "router_b"],
        "scale": a[L0 + "scale"],
        "w_in": low_layout(a[L1 + "W_in"].T, 2 * DI).T,
        "gamma": a[L1 + "gamma"][:, None],
        "beta": a[L1 + "beta"][:, None],
        "conv_w": a[L1 + "conv_w"].T.reshape(-1),
        "conv_b": a[L1 + "conv_b"][:, None],
        "w_x": a[L1 + "W_xproj"],
        "w_xT": a[L1 + "W_xproj"][:, :RANK].T,
        "w_dt": a[L1 + "W_dt"],
        "b_dt": a[L1 + "b_dt"][:, None],
        "a_log": a[L1 + "A_log"].reshape(NT, P).T,
        "d": a[L1 + "D"][:, None],
        "w_out": a[L1 + "W_out"],
        "w_out_low": low_layout(a[L1 + "W_out"], DI)[P:2 * P],
    }
    laid.update(selectors())
    nc = _bacc.Bacc("TRN2", target_bir_lowering=False, num_devices=1)
    arrays, A = {}, {}
    for name, v in laid.items():
        v = np.ascontiguousarray(v)
        arrays[f"in_{name}"] = v
        A[name] = nc.dram_tensor(f"in_{name}", v.shape, mybir.dt.from_np(v.dtype), kind="ExternalInput").ap()
    A["out"] = nc.dram_tensor("out", [IMGS, C, PIX], mybir.dt.float32, kind="ExternalOutput").ap()
    moe_mamba(nc, A)
    r = _run(nc, [arrays], core_ids=[0])
    return r.results[0]["out"].reshape(IMGS, C, 64, 64)
```

```python
import concourse.bass as bass
from concourse import mybir
from contextlib import ExitStack
import numpy as np

IMGS, C, PIX = 8, 96, 4096
E, HID = 4, 192
DI, NST, RANK, TAPS = 192, 16, 6, 4
P = 128
CH = 512
NCH = PIX // CH
NT = DI * NST // P
CPT = P // NST
HT = E * HID // P
GRP = 32
NG = DI // GRP
DR = DI - P
BLK = IMGS * PIX // P
WIN = CH + 2 * (TAPS - 1)
PADW = PIX + 2 * (TAPS - 1)
BODIES = 2 * NCH
LN_EPS = 1e-5
BATCH = 4
NB = NT // BATCH
LEAD_DT, LEAD_DTX = 5, 2
RING = 3

QUART = DR // 4
TILES = [(P + QUART * j + CPT * r, (QUART * j // CPT + r) % 4, r, j) for r in range(QUART // CPT) for j in range(4)]
LOW_BATCHES = len(TILES) // BATCH
TILES += [(GRP * j + CPT * r, r, r, j) for r in range(GRP // CPT) for j in range(4)]

GATES = ([(18, 0), (19, 1), (20, 2)], [(1, 3), (2, 4), (3, 5)])


def project_slot(odd, next_rev, fin):
    return 15 + (next_rev or fin) if odd else 14 + fin


def ring(odd):
    out = []
    for i in range(NT):
        out += [("gate", m) for slot, m in GATES[odd] if slot == i - 1] + [("tile", i)]
    assert len(out) % RING == 0 and all(kind == "tile" for kind, _ in out[-RING:])
    return out


def selectors():
    sel = np.zeros((3 * GRP, 4, P), np.float32)
    red = np.zeros((P, 4, GRP), np.float32)
    for p in range(P):
        for r in range(4):
            sel[CPT * r + p // NST::GRP, r, p] = 1
            red[p, r, CPT * r + p // NST] = 1
    gate = np.zeros((3 * E, HT, P), np.float32)
    for m in range(HT):
        for p in range(P):
            gate[(m * P + p) // HID::E, m, p] = 1
    return {
        "c_sel": sel.reshape(3 * GRP, -1), "c_red": red.reshape(P, -1), "c_gate": gate.reshape(3 * E, -1),
        "c_ident": np.eye(P, dtype=np.float32), "c_mean": np.full((C, C), 1.0 / C, np.float32),
    }


def bank_uses(odd, next_rev, fin):
    out, z0, z1 = [("OUT", 0)] if fin else [], [("Z0", 1 - odd)] if next_rev else [], [("Z1", 1)] if next_rev else []
    if odd:
        return ([("D0", 0), ("D1", 1), ("C", 0), ("Y2", 1)] + out + [("MU", 1)] + z0
                + [("VAR", 1), ("U0", 0), ("U1", 1)] + z1)
    return ([("D0", 0), ("D1", 1), ("GT", 0)] + [(f"H{m}", 1 - m % 2) for m in range(HT)] + [("C", 1)] + out + z0
            + [("U0", 0), ("U1", 1)] + z1)


def count(uses, bank):
    return sum(b == bank for _, b in uses)


class Uses:

    def __init__(self, uses, base):
        self.at, seen = {}, [0, 0]
        for name, bank in uses:
            self.at[name] = (bank, base[bank] + seen[bank])
            seen[bank] += 1


PRO_PIECE = [("GT", 1)] + [(f"H{m}", m % 2) for m in range(HT)] + [("Y2", 1), ("MU", 1), ("VAR", 0)]
PRO_U = [("U0", 0), ("U1", 1)]
PRO_D = [("D0", 0), ("D1", 1), ("C", 0)]
PRO = [count(PRO_PIECE, i) * NCH + 2 * count(PRO_U, i) + count(PRO_D, i) for i in (0, 1)]


def prologue_uses():
    at = [count(PRO_PIECE, i) * NCH for i in (0, 1)]
    out = []
    for uses in (PRO_U, PRO_U, PRO_D):
        out.append(Uses(uses, at))
        at = [at[i] + count(uses, i) for i in (0, 1)]
    return out


def piece_uses(j):
    return Uses(PRO_PIECE, [j * count(PRO_PIECE, i) for i in (0, 1)])


def kinds():
    half = NCH // 2
    return [(0, 0, 1, False, None), (0, 1, half - 2, False, 0), (0, half - 1, 1, True, 0),
            (1, 0, 1, False, 0), (1, 1, half - 2, False, 1), (1, half - 1, 1, True, 1)]


def pair_uses(run):
    rev, _, _, last, before = run
    return (bank_uses(False, rev == 1, before == 1), bank_uses(True, (rev == 1) != last, rev == 1))


TAIL = [("OUT", 0)]
PER_IMAGE = [sum(n * (count(a, i) + count(b, i)) for run in kinds() for n in [run[2]] for a, b in [pair_uses(run)])
             + count(TAIL, i) for i in (0, 1)]


def bodies(eng, body, tail):
    with eng.Fori(0, IMGS) as img:
        start = [PRO[i] + img * PER_IMAGE[i] for i in (0, 1)]
        for run in kinds():
            rev, p0, pairs, last, before = run
            even, odd = pair_uses(run)
            per = [count(even, i) + count(odd, i) for i in (0, 1)]

            def pair(q):
                base = [start[i] + (q - p0) * per[i] for i in (0, 1)]
                body(img, q, rev, 0, last, before, Uses(even, base))
                base = [base[i] + count(even, i) for i in (0, 1)]
                body(img, q, rev, 1, last, rev, Uses(odd, base))

            if pairs > 1:
                with eng.Fori(p0, p0 + pairs) as q:
                    pair(q)
            else:
                pair(p0)
            start = [start[i] + pairs * per[i] for i in (0, 1)]
        tail(img, Uses(TAIL, start))


def chunk_of(q, rev, odd):
    return (NCH - 1 - odd) - q * 2 if rev else q * 2 + odd


def moe_mamba(nc, A):
    f32, bf16 = mybir.dt.float32, mybir.dt.bfloat16
    ALU, ACT, AX = mybir.AluOpType, mybir.ActivationFunctionType, mybir.AxisListType
    ctx = ExitStack()
    with ctx:
        def sb(name, shape, dt=f32):
            return ctx.enter_context(nc.sbuf_tensor(name, shape, dt))

        def sem(name):
            return ctx.enter_context(nc.semaphore(name))

        xn_d = nc.dram_tensor("xn_d", [IMGS, C + 1, PADW], f32, kind="Internal").ap()
        x2_d = nc.dram_tensor("x2_d", [IMGS, C, PIX], f32, kind="Internal").ap()

        w1 = sb("w1", [C, E * HID])
        w2 = sb("w2", [P, HT, C])
        b1 = sb("b1", [P, HT])
        b2f = sb("b2f", [3 * E, C])
        b2r = sb("b2r", [3 * E, C])
        b2s = sb("b2s", [3 * E, 3, C], bf16)
        scl = sb("scl", [P, 1])
        wr = sb("wr", [C, E])
        rb = sb("rb", [P, E])
        w_in = sb("w_in", [C, DI + 2 * P])
        w_g = sb("w_g", [C + 1, DI + 2 * P])
        gam = sb("gam", [C, 1])
        bet = sb("bet", [C, 1])
        w_u = sb("w_u", [C + 1, TAPS, DI])
        cb = [sb("cb0", [P, 1]), sb("cb1", [DR, 1])]
        wx = [sb("wx0", [P, RANK + 2 * NST]), sb("wx1", [DR, RANK + 2 * NST])]
        wxT = sb("wxT", [RANK, DI])
        wdt = sb("wdt", [RANK, DI])
        w_d = [sb("wd0", [P, 2 * P]), sb("wd1", [DR, 2 * P])]
        w_c = [sb("wc0", [P, P]), sb("wc1", [DR, P])]
        bd = [sb("bd0", [P, 1]), sb("bd1", [DR, 1])]
        amat = sb("amat", [P, NT])
        dvec = [sb("dv0", [P, 1]), sb("dv1", [DR, 1])]
        diag = [sb("dg0", [P, P]), sb("dg1", [DR, P])]
        wo0 = sb("wo0", [P, C])
        wo1 = sb("wo1", [P, C])
        sel = sb("sel", [3 * GRP, 4, P], bf16)
        red = sb("red", [P, 4, GRP])
        gsel = sb("gsel", [3 * E, HT, P], bf16)
        ident = sb("ident", [P, P])
        identb = sb("identb", [P, P], bf16)
        mean = sb("mean", [C, C])
        konst = sb("konst", [P, 1])
        EPS = konst[:, 0:1]

        g3 = sb("g3", [P, BLK, 3 * E], bf16)
        gT = sb("gT", [3 * E, CH], bf16)
        xp = sb("xp", [C, CH])
        hid = sb("hid", [P, HT, CH])
        x2p = sb("x2p", [C, CH])
        xc = sb("xc", [C, CH])
        sq = sb("sq", [C, CH])
        xnp = sb("xnp", [C, CH])

        win = sb("win", [C + 1, 2, WIN])
        xr = [sb("xr0", [P, 2, CH]), sb("xr1", [DR, 2, CH])]
        S = sb("S", [P, 3, CH])
        spl = sb("spl", [P, 3, 3, CH], bf16)
        pk = sb("pk", [3 * GRP, 2, 2, NG, CH], bf16)
        bB = sb("bB", [P, 2, CH])
        cC = sb("cC", [P, 2, CH])
        dA = sb("dA", [P, 6, CH])
        h = sb("h", [P, 8, CH])
        hc = sb("hc", [P, 8, CH])
        carry = sb("carry", [P, NT])
        ys0 = sb("ys0", [P, PIX])
        ys1 = sb("ys1", [P, PIX])
        yr0 = sb("yr0", [P, CH])
        yr1 = sb("yr1", [P, 2, CH])
        rl1 = sb("rl1", [DR, CH])
        sz0 = sb("sz0", [P, 2, CH])
        sz1 = sb("sz1", [P, 2, CH])
        xf = sb("xf", [C, CH])
        NA, NH = 6, 8

        ps = [ctx.enter_context(nc.psum_tensor(f"ps{i}", [P, CH], f32)) for i in range(8)]
        p_dt, p_ring, p_y, p_w = ps[0:2], ps[2:5], ps[5], ps[6:8]

        s_ld = sem("weights_loaded")
        s_cst = sem("setup_vector")
        s_setup_pe = sem("setup_tensor")
        s_setup_act = sem("setup_scalar")
        s_ready = sem("setup_done")
        s_xl = [sem("router_x_loaded0"), sem("router_x_loaded1")]
        s_rt = sem("router_logits")
        s_rc = sem("router_copied")
        s_gm = sem("gate_math")
        s_ge = sem("gate_exp")
        s_pad = sem("padding_stored")
        s_dt = sem("dt_broadcast")
        s_exp = sem("dA_ready")
        s_dtx = sem("dtx_broadcast")
        s_gelu = sem("gelu_done")
        s_gr = sem("gate_rows")
        s_gated = sem("hidden_gated")
        s_mul = sem("dBx_ready")
        s_scan = sem("h_ready")
        s_hc = sem("hC_ready")
        s_carry = sem("carry_ready")
        s_y = sem("y_summed")
        s_ev = sem("y_evacuated")
        s_pr = [sem("work_bank0_ready"), sem("work_bank1_ready")]
        s_pf = [sem("work_bank0_free"), sem("work_bank1_free")]
        s_sp = [sem("softplus_steps0"), sem("softplus_steps1")]
        s_dts = [sem("dt_ready0"), sem("dt_ready1")]
        s_s = sem("dtx_ready")
        s_cast = sem("split_cast")
        s_r1 = sem("split_rest")
        s_lo = sem("split_low")
        s_pk = sem("packed")
        s_b = sem("b_copied")
        s_win = [sem("window0_loaded"), sem("window1_loaded")]
        s_met = sem("waits_met")
        s_xp = sem("piece_loaded")
        s_sqr = sem("ln_square")
        s_rs = sem("ln_rstd")
        s_xn = sem("ln_done")
        s_x2s = sem("x2_stored")
        s_xns = sem("xn_stored")
        s_fin = sem("gated_y")
        s_xf = sem("residual_loaded")
        s_out = sem("out_stored")

        PKB = 16 * 24

        block = ctx.enter_context(nc.Block())


        def body_number(img, q, rev, odd):
            return img * BODIES + q * 2 + (NCH * rev + odd)

        def piece_number(img, q, rev):
            return NCH + img * NCH + q + (NCH // 2) * rev

        def next_image(img):
            return (img + 1) % IMGS

        @block.sync
        def _(sp):
            def wait_then_address(semaphore, value):
                sp.wait_ge(s_ld, 16 * N_LOADS)
                sp.wait_ge(semaphore, value)

            def wait_alone(semaphore, value):
                sp.wait_ge(semaphore, value)
                sp.sem_inc(s_met, 1)

            loads = [
                (w1[:, :], A["w1T"]), (w2[:, :, :], A["w2T"]), (b1[:, :], A["b1"]), (b2f[:, :], A["b2"]),
                (wr[:, :], A["wrT"]), (w_in[:, :], A["w_in"]), (gam[:, :], A["gamma"]), (bet[:, :], A["beta"]),
                (cb[0][:, :], A["conv_b"][0:P, :]), (cb[1][:, :], A["conv_b"][P:DI, :]),
                (wx[0][:, :], A["w_x"][0:P, :]), (wx[1][:, :], A["w_x"][P:DI, :]), (wxT[:, :], A["w_xT"]),
                (wdt[:, :], A["w_dt"]), (bd[0][:, :], A["b_dt"][0:P, :]), (bd[1][:, :], A["b_dt"][P:DI, :]),
                (amat[:, :], A["a_log"]), (dvec[0][:, :], A["d"][0:P, :]), (dvec[1][:, :], A["d"][P:DI, :]),
                (wo0[:, :], A["w_out"][0:P, :]), (wo1[:, :], A["w_out_low"]),
                (red[:, :, :], A["c_red"].rearrange("p (r c) -> p r c", r=4)), (ident[:, :], A["c_ident"]),
                (mean[:, :], A["c_mean"]),
                (hid[0:3 * GRP, 0, :], A["c_sel"]),
                (hid[0:3 * E, 1, :], A["c_gate"][:, 0:CH]), (hid[0:3 * E, 2, 0:HT * P - CH], A["c_gate"][:, CH:HT * P]),
                (scl[:, :], A["scale"].partition_broadcast(P)), (rb[:, :], A["router_b"].partition_broadcast(P)),
                (ys0[0:C + 1, 0:TAPS * DI], A["conv_w"].partition_broadcast(C + 1)),
            ]
            for credit in (s_x2s, s_xns, s_out):
                sp.sem_inc(credit, 16)
            for out, src in loads:
                sp.dma_start(out, src).then_inc(s_ld, 16)
            assert len(loads) == N_LOADS
            HALF = PIX // 2
            with sp.Fori(0, IMGS) as i:
                for half in range(2):
                    wait_alone(s_rt, i * 2 + half + 1)
                    for k in range(4 * half, 4 * half + 4):
                        sp.dma_start(hc[0:C, k, :], A["x"][bass.ds(i, 1), :, k * CH:(k + 1) * CH].rearrange("o c t -> (o c) t")
                                     ).then_inc(s_xl[half], 16)
            sp.wait_ge(s_ready, 1)

            def copy_b(par):
                sp.dma_start(bB[0:DR, par, :], bB[DR:P, par, :]).then_inc(s_b, 16)

            def load_piece(image, j, pc):
                wait_then_address(s_xn, pc + 1)
                sp.dma_start(xp[:, :], A["x"][bass.ds(image, 1), :, bass.ds(j * CH, CH)].rearrange("o c t -> (o c) t")).then_inc(s_xp, 16)

            def store_x2(image, j, pc, u):
                bank, at = u.at["Y2"]
                wait_then_address(s_pf[bank], at + 2)
                sp.dma_start(x2_d[bass.ds(image, 1), :, bass.ds(j * CH, CH)].rearrange("o c t -> (o c) t"), x2p[:, :]).then_inc(s_x2s, 16)

            def store_xn(image, j, pc):
                wait_then_address(s_xn, pc + 2)
                sp.dma_start(xn_d[bass.ds(image, 1), 0:C, bass.ds(TAPS - 1 + j * CH, CH)].rearrange("o c t -> (o c) t"), xnp[:, :]).then_inc(s_xns, 16)

            def load_window(image, chunk, par, pieces):
                if pieces is not None:
                    wait_then_address(s_xns, pieces * 16 + 16)
                sp.dma_start(win[:, par, :], xn_d[bass.ds(image, 1), :, bass.ds(chunk * CH, WIN)].rearrange("o c t -> (o c) t")).then_inc(s_win[par], 16)

            def pack(part, par):
                rows = slice(GRP * part, GRP * part + GRP)
                for g in range(4):
                    sp.dma_start(pk[rows, par, :, g, :], spl[GRP * g:GRP * g + GRP, part, 0:2, :]).then_inc(s_pk, 16)
                for k in range(4):
                    sp.dma_start(pk[rows, par, k // 2, 4 + k % 2, :], spl[GRP * k:GRP * k + GRP, part, 2, :]).then_inc(s_pk, 16)

            assert IMGS == NCH
            with sp.Fori(0, NCH) as j:
                load_piece(0, j, j)
                for lo in (0, PADW - (TAPS - 1)):
                    sp.dma_start(xn_d[bass.ds(j, 1), :, lo:lo + TAPS - 1].rearrange("o c t -> (o c) t"),
                                 ys0[0:C + 1, 1024:1024 + TAPS - 1]).then_inc(s_pad, 16)
                for k in range(PIX // 1024):
                    sp.dma_start(xn_d[bass.ds(j, 1), C:C + 1, TAPS - 1 + 1024 * k:TAPS - 1 + 1024 * (k + 1)].rearrange("o c t -> (o c) t"),
                                 ys0[0:1, 2048:3072]).then_inc(s_pad, 16)
                store_x2(0, j, j, piece_uses(j))
                store_xn(0, j, j)
            sp.wait_ge(s_pad, 16 * (2 + PIX // 1024) * IMGS)
            for c in range(2):
                load_window(0, c, c, NCH)
            sp.wait_ge(s_cast, 1)
            copy_b(0)
            pack(0, 0)
            sp.wait_ge(s_cast, 2)
            pack(1, 0)
            sp.wait_ge(s_lo, 2)
            pack(2, 0)

            def store_out(img, chunk, at):
                wait_then_address(s_pf[0], at + 2)
                sp.dma_start(A["out"][bass.ds(img, 1), :, bass.ds(chunk * CH, CH)].rearrange("o c t -> (o c) t"), xf[:, :]).then_inc(s_out, 16)

            def load_residual(img, chunk, f):
                wait_alone(s_x2s, (img + 1) * (NCH * 16) + 16)
                wait_alone(s_out, f * 16 + 16)
                sp.dma_start(xf[:, :], x2_d[bass.ds(img, 1), :, bass.ds(chunk * CH, CH)].rearrange("o c t -> (o c) t")).then_inc(s_xf, 16)

            def body(img, q, rev, odd, last, before, u):
                fin = before == 1
                n, pc = body_number(img, q, rev, odd), piece_number(img, q, rev)
                par, j = odd, q + (NCH // 2) * rev
                nimg = next_image(img)
                wait_alone(s_dt, n * NT + LEAD_DT)
                if last and rev:
                    pass
                elif last:
                    load_window(img, NCH - 1 - odd, par, None)
                else:
                    load_window(img, chunk_of(q, rev, odd) + (-2 if rev else 2), par, None if rev else (img + 1) * NCH)
                if not odd:
                    load_piece(nimg, j, pc)
                if fin:
                    load_residual(img, chunk_of(q, rev, odd) + 1, img * NCH + q * 2 + odd - 1)
                if last and rev:
                    sp.wait_ge(s_xns, ((img + 1) * NCH + (NCH // 2)) * 16 + 16)
                sp.wait_ge(s_cast, 2 * n + 3)
                copy_b(1 - par)
                pack(0, 1 - par)
                if last and rev:
                    load_window(nimg, odd, par, None)
                if fin:
                    store_out(img, chunk_of(q, rev, odd) + 1, u.at["OUT"][1])
                sp.wait_ge(s_cast, 2 * n + 4)
                pack(1, 1 - par)
                sp.wait_ge(s_lo, n + 3)
                pack(2, 1 - par)
                if odd:
                    store_x2(nimg, j, pc, u)
                    store_xn(nimg, j, pc)

            def tail(img, u):
                load_residual(img, 0, img * NCH + (NCH - 1))
                store_out(img, 0, u.at["OUT"][1])

            bodies(sp, body, tail)
            sp.wait_ge(s_out, 16 * IMGS * NCH + 16)
            sp.wait_ge(s_x2s, 16 * NCH * (IMGS + 1) + 16)
            sp.wait_ge(s_xns, 16 * NCH * (IMGS + 1) + 16)
            for k in range(2):
                sp.wait_ge(s_win[k], 16 * (IMGS * BODIES // 2 + 1))
            sp.wait_ge(s_pk, PKB * (IMGS * BODIES + 1))
            sp.wait_ge(s_b, 16 * (IMGS * BODIES + 1))

        @block.tensor
        def _(pe):
            mm = nc.tensor.matmul
            pe.wait_ge(s_ld, 16 * N_LOADS)
            mm(ps[0][0:1, 0:DI + 2 * P], bet[:, :], w_in[:, :], start=True, stop=True).then_inc(s_setup_pe, 1)
            mm(ps[1][:, 0:DI], wxT[:, 0:P], wdt[:, :], start=True, stop=True).then_inc(s_setup_pe, 1)
            mm(ps[2][0:DR, 0:DI], wxT[:, P:DI], wdt[:, :], start=True, stop=True).then_inc(s_setup_pe, 1)
            pe.sem_inc(s_rt, 2)
            with pe.Fori(0, IMGS) as i:
                for half in range(2):
                    pe.wait_ge(s_xl[half], i * 64 + 64)
                    pe.wait_ge(s_rc, i * 2 + half + 1)
                    for b in range(16):
                        last = mm(ps[6 + half][:, E * b:E * b + E], hc[0:C, 4 * half + b // 4, P * (b % 4):P * (b % 4) + P],
                                  wr[:, :], start=True, stop=True)
                    last.then_inc(s_rt, 1)

            def begin(u, name):
                bank, at = u.at[name]
                pe.wait_ge(s_pf[bank], at + 1)
                return p_w[bank]

            def ready(u, name, last):
                last.then_inc(s_pr[u.at[name][0]], 1)

            def gates_transposed(image, j, u):
                out = begin(u, "GT")
                for s in range(4):
                    last = mm(out[0:3 * E, P * s:P * s + P],
                              g3[:, bass.ds(image * (PIX // P) + (j * 4 + s), 1), :].rearrange("p o e -> p (o e)"),
                              identb[:, :], start=True, stop=True)
                ready(u, "GT", last)

            def hidden(m, pc, u):
                if m == 0:
                    pe.wait_ge(s_xp, pc * 16 + 16)
                ready(u, f"H{m}", mm(begin(u, f"H{m}")[:, :], w1[:, P * m:P * m + P], xp[:, :], start=True, stop=True))

            def gate_rows(m, pc, bank, gt):
                bk, at = gt.at["GT"]
                pe.wait_ge(s_pf[bk], at + 2)
                mm(p_ring[bank][:, :], gsel[:, m, :], gT[:, :], start=True, stop=True).then_inc(s_gr, 1)

            def expert_out(m, u, pc):
                if m == 0:
                    begin(u, "Y2")
                pe.wait_ge(s_gated, pc * HT + (m + 1 + RING))
                mm(p_w[1][0:C, :], w2[:, m, :], hid[:, m, :], start=(m == 0), stop=False)

            def expert_bias(u):
                for s in range(3):
                    last = mm(p_w[1][0:C, :], b2s[:, s, :], gT[:, :], start=False, stop=(s == 2))
                ready(u, "Y2", last)

            def ln_mean(u):
                pe.wait_ge(s_pf[1], u.at["Y2"][1] + 2)
                ready(u, "MU", mm(begin(u, "MU")[0:C, :], mean[:, :], x2p[:, :], start=True, stop=True))

            def ln_var(pc, u):
                pe.wait_ge(s_sqr, pc + 1)
                ready(u, "VAR", mm(begin(u, "VAR")[0:C, :], mean[:, :], sq[:, :], start=True, stop=True))

            def project(half, taps, par, rev, u):
                name, lo, m = f"U{half}", P * half, (P, DR)[half]
                for t in taps:
                    if t == 0:
                        begin(u, name)
                    at = 2 * (TAPS - 1) - t if rev else t
                    last = mm(p_w[half][0:m, :], w_u[:, t, lo:lo + m], win[:, par, at:at + CH],
                              start=(t == 0), stop=(t == TAPS - 1))
                    if t == TAPS - 1:
                        ready(u, name, last)

            def project_z(half, par, u):
                lo = DI + P * half
                ready(u, f"Z{half}", mm(begin(u, f"Z{half}")[:, :], w_g[:, lo:lo + P], win[:, par, TAPS - 1:TAPS - 1 + CH],
                                        start=True, stop=True))

            def from_xr(name, w, par, u):
                out = begin(u, name)
                mm(out[:, :], w[0], xr[0][:, par, :], start=True, stop=False)
                ready(u, name, mm(out[:, :], w[1], xr[1][:, par, :], start=False, stop=True))

            def project_dt(half, par, u):
                from_xr(f"D{half}", [w[:, P * half:P * half + P] for w in w_d], par, u)

            def project_c(par, u):
                from_xr("C", [w[:, :] for w in w_c], par, u)

            def bc(which, dst, i, par):
                ch, r, _, _ = TILES[i]
                return mm(dst[:, :], sel[:, r, :], pk[:, par, which, ch // GRP, :], start=True, stop=True)

            def bc_dt(n, i, par):
                if i == 0:
                    pe.wait_ge(s_pk, (n + 1) * PKB)
                pe.wait_ge(s_exp, n * NT + (i + 1))
                bc(0, p_dt[i % 2], i, par).then_inc(s_dt, 1)

            def through_ring(n, pc, odd, upto, gt):
                elements = ring(odd)
                k1 = elements.index(("tile", upto))
                k0 = elements.index(("tile", upto - 1)) + 1 if upto else 0
                for k in range(k0, k1 + 1):
                    was, at = elements[k - RING] if k >= RING else ("tile", NT - RING + k - NT)
                    if was == "tile":
                        pe.wait_ge(s_scan, n * NT + (at + 1 + 8))
                    else:
                        pe.wait_ge(s_gated, pc * HT + (at + 1 + RING))
                    kind, at = elements[k]
                    if kind == "tile":
                        bc(1, p_ring[k % RING], at, odd).then_inc(s_dtx, 1)
                    else:
                        gate_rows(at, pc, k % RING, gt)

            def d_times_x(n, low, par):
                pe.wait_ge(s_ev, n * 2 + (2 if low else 3))
                k = 1 if low else 0
                mm(p_y[:, :], diag[k][:, :], xr[k][:, par, :], start=True, stop=False, skip_group_check=True)

            def sum_states(n, r):
                pe.wait_ge(s_hc, n * NT + (BATCH * (r + 1) + 8))
                for i in range(BATCH * r, BATCH * r + BATCH):
                    _, _, row, col = TILES[i]
                    last = mm(p_y[GRP * col:GRP * col + GRP, :], red[:, row, :], hc[:, i % NH, :], start=False,
                              stop=(r in (LOW_BATCHES - 1, NB - 1)), skip_group_check=True)
                last.then_inc(s_y, 1)

            def finish(u, f, par):
                pe.wait_ge(s_fin, f * 4 + 4)
                out = begin(u, "OUT")
                mm(out[0:C, :], wo0[:, :], yr0[:, :], start=True, stop=False)
                ready(u, "OUT", mm(out[0:C, :], wo1[:, :], yr1[:, par, :], start=False, stop=True))

            pe.wait_ge(s_ready, 1)
            with pe.Fori(0, NCH) as j:
                u = piece_uses(j)
                gates_transposed(0, j, u)
                for m in range(HT):
                    hidden(m, j, u)
                for m in range(HT):
                    pe.wait_ge(s_gated, j * HT + (m + 1))
                    gate_rows(m, j, m % RING, u)
                for m in range(HT):
                    expert_out(m, u, j)
                expert_bias(u)
                ln_mean(u)
                ln_var(j, u)
            first, second, rest = prologue_uses()
            for par, u in ((0, first), (1, second)):
                pe.wait_ge(s_win[par], 16)
                for half in range(2):
                    project(half, range(TAPS), par, 0, u)
            for k in range(2):
                bank, at = second.at[f"U{k}"]
                pe.wait_ge(s_pf[bank], at + 2)
            project_dt(0, 0, rest)
            project_dt(1, 0, rest)
            project_c(0, rest)
            for i in range(LEAD_DT):
                bc_dt(0, i, 0)
            for i in range(LEAD_DTX):
                through_ring(0, 0, 0, i, None)

            even = [None]

            def body(img, q, rev, odd, last, before, u):
                fin = before == 1
                n, pc = body_number(img, q, rev, odd), piece_number(img, q, rev)
                par, nxt, j = odd, 1 - odd, q + (NCH // 2) * rev
                nrev = (rev == 1) != (last and odd == 1)
                urev = (rev == 1) != last
                nimg = next_image(img)
                gt = even[0] if odd else u
                if not odd:
                    even[0] = u

                for i in range(NT):
                    if i + LEAD_DT < NT:
                        bc_dt(n, i + LEAD_DT, par)
                    else:
                        bc_dt(n + 1, i + LEAD_DT - NT, nxt)
                    if i + LEAD_DTX < NT:
                        through_ring(n, pc, odd, i + LEAD_DTX, gt)
                    else:
                        through_ring(n + 1, pc, nxt, i + LEAD_DTX - NT, gt)
                    if i == 0:
                        project_dt(0, nxt, u)
                    if i == 1:
                        project_dt(1, nxt, u)
                    if i == (3 if odd else 11):
                        project_c(nxt, u)
                    if i == 12 and fin:
                        finish(u, img * NCH + q * 2 + odd - 1, nxt)
                    first = project_slot(odd, nrev, fin)
                    if i == first:
                        pe.wait_ge(s_win[par], (img * (BODIES // 2) + q + ((NCH // 2) * rev + 2)) * 16)
                    if first <= i < first + 4:
                        k = i - first
                        project(k // 2, (2 * (k % 2), 2 * (k % 2) + 1), par, urev, u)
                    if i == 13 + odd and nrev:
                        project_z(0, nxt, u)
                    if i == 21 and nrev:
                        project_z(1, nxt, u)
                    if not odd:
                        if i == 3:
                            gates_transposed(nimg, j, u)
                        if i in range(5, 5 + HT):
                            hidden(i - 5, pc, u)
                    else:
                        if i in range(4, 4 + HT):
                            expert_out(i - 4, u, pc)
                        if i == 10:
                            expert_bias(u)
                        if i == 12:
                            ln_mean(u)
                        if i == 14:
                            ln_var(pc, u)
                    if i == 6:
                        d_times_x(n, True, par)
                    if i == 13:
                        d_times_x(n, False, par)
                    if i == 2 and before is not None:
                        sum_states(n - 1, NB - 1)
                    if i % BATCH == 2 and i >= 6:
                        sum_states(n, (i - 6) // BATCH)

            def tail(img, u):
                sum_states((img + 1) * BODIES - 1, NB - 1)
                finish(u, img * NCH + (NCH - 1), 1)

            bodies(pe, body, tail)

        @block.scalar
        def _(act):
            A_ = nc.scalar.activation
            act.sem_inc(s_exp, 2)
            act.sem_inc(s_ev, 2)
            act.sem_inc(s_pf[0], 1)
            act.sem_inc(s_pf[1], 1)
            act.wait_ge(s_setup_pe, 3)
            A_(w_g[C:C + 1, :], ps[0][0:1, 0:DI + 2 * P], ACT.Copy).then_inc(s_setup_act, 1)
            A_(w_d[0][:, 0:DI], ps[1][:, 0:DI], ACT.Copy).then_inc(s_setup_act, 1)
            A_(w_d[1][:, 0:DI], ps[2][0:DR, 0:DI], ACT.Copy).then_inc(s_setup_act, 1)
            A_(amat[:, :], amat[:, :], ACT.Exp).then_inc(s_setup_act, 1)
            act.wait_ge(s_gm, 1)
            A_(dA[:, 0:2, :], dA[:, 0:2, :], ACT.Exp).then_inc(s_ge, 1)
            act.wait_ge(s_ready, 1)

            def begin(u, name):
                bank, at = u.at[name]
                act.wait_ge(s_pr[bank], at + 1)
                return p_w[bank]

            def free(u, name, ins):
                ins.then_inc(s_pf[u.at[name][0]], 1)

            def main_tables():
                nc.scalar.preload_act_table_set("natural_log_exp_and_others")

            def copy_gates(u):
                free(u, "GT", A_(gT[:, :], begin(u, "GT")[0:3 * E, :], ACT.Copy))

            def copy_hidden(m, u):
                free(u, f"H{m}", A_(hid[:, m, :], begin(u, f"H{m}")[:, :], ACT.Copy))

            def gelu(u):
                for m in range(HT):
                    bank, at = u.at[f"H{m}"]
                    act.wait_ge(s_pf[bank], at + 2)
                    A_(hid[:, m, :], hid[:, m, :], ACT.Gelu, bias=b1[:, m:m + 1]).then_inc(s_gelu, 1)
                main_tables()

            def ln_square(u, pc):
                act.wait_ge(s_pf[1], u.at["MU"][1] + 2)
                A_(sq[:, :], xc[:, :], ACT.Square).then_inc(s_sqr, 1)

            def ln_rstd(u, pc):
                out = begin(u, "VAR")
                free(u, "VAR", A_(sq[:, :], out[0:C, :], ACT.Ln, bias=EPS[0:C, :]))
                bank, at = u.at["VAR"]
                act.wait_ge(s_pf[bank], at + 2)
                A_(sq[:, :], sq[:, :], ACT.Exp, scale=-0.5).then_inc(s_rs, 1)

            def silu_x(u, par):
                for k, m in enumerate((P, DR)):
                    free(u, f"U{k}", A_(xr[k][:, par, :], begin(u, f"U{k}")[0:m, :], ACT.Silu, bias=cb[k][:, :]))

            def silu_z(n, cpar):
                act.wait_ge(s_exp, n * NT + (LEAD_DT + 1 + 2))
                A_(sz0[:, cpar, :], sz0[:, cpar, :], ACT.Silu)
                A_(sz1[:, cpar, :], sz1[:, cpar, :], ACT.Silu)

            def copy_z(half, u, cpar, f):
                out = begin(u, f"Z{half}")
                if f is not None and half == 0:
                    act.wait_ge(s_fin, f * 4 + 4)
                free(u, f"Z{half}", A_((sz1 if half else sz0)[:, cpar, :], out[:, :], ACT.Copy))

            SP_LOG = (S[:, 0, :], S[0:DR, 2, :])
            SP_RELU = (S[:, 1, :], rl1[:, :])
            ROWS_OF = (P, DR)

            def sp_abs(k, u, b):
                if k == 0:
                    act.wait_ge(s_lo, b + 1)
                A_(SP_LOG[k], begin(u, f"D{k}")[0:ROWS_OF[k], :], ACT.Abs, bias=bd[k][:, :]).then_inc(s_sp[k], 1)

            def sp_relu(k, u):
                free(u, f"D{k}", A_(SP_RELU[k], p_w[k][0:ROWS_OF[k], :], ACT.Relu, bias=bd[k][:, :]))

            def sp_exp(k, b):
                act.wait_ge(s_sp[k], b * 3 + 1)
                A_(SP_LOG[k], SP_LOG[k], ACT.Exp, scale=-1.0).then_inc(s_sp[k], 1)

            def sp_log(k, b):
                act.wait_ge(s_sp[k], b * 3 + 2)
                A_(SP_LOG[k], SP_LOG[k], ACT.Ln, bias=1.0).then_inc(s_sp[k], 1)

            def copy_b(par):
                A_(bB[DR:P, par, :], p_w[1][DR:P, :], ACT.Copy)

            def copy_c(u, par):
                free(u, "C", A_(cC[:, par, :], begin(u, "C")[:, :], ACT.Copy))

            def cast_high(b):
                act.wait_ge(s_s, b * 2 + 2)
                if not isinstance(b, int):
                    act.wait_ge(s_pk, b * PKB)
                A_(spl[:, 0, :, :], S[:, :, :], ACT.Copy).then_inc(s_cast, 1)

            def cast_mid(b):
                act.wait_ge(s_r1, b + 2)
                A_(spl[:, 1, :, :], S[:, :, :], ACT.Copy).then_inc(s_cast, 1)

            def exp_dA(n, i):
                act.wait_ge(s_dt, n * NT + (i + 1))
                act.wait_ge(s_scan, n * NT + (i - NA + 1 + 8))
                col = TILES[i][0] // CPT
                A_(dA[:, i % NA, :], p_dt[i % 2][:, :], ACT.Exp, scale=amat[:, col:col + 1]).then_inc(s_exp, 1)

            def evacuate(n, low, rev, chunk, par):
                act.wait_ge(s_y, n * NB + (2 + (LOW_BATCHES if low else NB)))
                if rev:
                    dst = yr1[:, par, :] if low else yr0[:, :]
                else:
                    dst = (ys1 if low else ys0)[:, bass.ds(chunk * CH, CH)]
                A_(dst, p_y[:, :], ACT.Copy).then_inc(s_ev, 1)

            with act.Fori(0, NCH) as j:
                u = piece_uses(j)
                copy_gates(u)
                for m in range(HT):
                    copy_hidden(m, u)
                gelu(u)
                ln_square(u, j)
                ln_rstd(u, j)
            first, second, rest = prologue_uses()
            silu_x(first, 0)
            silu_x(second, 1)
            main_tables()
            for k in range(2):
                sp_abs(k, rest, 0)
                if k == 1:
                    copy_b(0)
                sp_relu(k, rest)
                sp_exp(k, 0)
                sp_log(k, 0)
            copy_c(rest, 0)
            cast_high(0)
            cast_mid(0)
            for i in range(LEAD_DT):
                exp_dA(0, i)

            def body(img, q, rev, odd, last, before, u):
                fin = before == 1
                n, pc = body_number(img, q, rev, odd), piece_number(img, q, rev)
                nxt = 1 - odd
                nrev = (rev == 1) != (last and odd == 1)
                f = img * NCH + q * 2 + odd - 1 if fin else None
                z_at = (14 + odd, 22)
                for i in range(NT):
                    exp_dA(*((n, i + LEAD_DT) if i + LEAD_DT < NT else (n + 1, i + LEAD_DT - NT)))
                    if i == 1:
                        sp_abs(0, u, n + 1)
                        sp_relu(0, u)
                    if i == 2:
                        sp_exp(0, n + 1)
                        sp_abs(1, u, n + 1)
                    if i == 3:
                        copy_b(nxt)
                        sp_relu(1, u)
                    if i == 4:
                        if before is not None:
                            evacuate(n - 1, False, before, q * 2 + odd - 1 + (NCH if before != rev else 0), nxt)
                        sp_log(0, n + 1)
                        sp_exp(1, n + 1)
                    if i == 5:
                        sp_log(1, n + 1)
                    if i == 9:
                        cast_high(n + 1)
                    if i == (8 if odd else 12):
                        copy_c(u, nxt)
                    if i == 12:
                        evacuate(n, True, rev, q * 2 + odd, odd)
                    if i == 13:
                        cast_mid(n + 1)
                    if i == project_slot(odd, nrev, fin) + 4 + (not (odd or fin)):
                        silu_x(u, odd)
                        if rev:
                            silu_z(n, 1 - odd)
                        main_tables()
                    if not odd:
                        if i == 4:
                            copy_gates(u)
                        if i in range(6, 6 + HT):
                            copy_hidden(i - 6, u)
                    elif i == 14:
                        ln_square(u, pc)
                    if nrev and i in z_at:
                        copy_z(z_at.index(i), u, 1 - nxt, f)
                    if not odd and i == 14:
                        gelu(u)
                    if odd and i == 16:
                        ln_rstd(u, pc)

            def tail(img, u):
                evacuate((img + 1) * BODIES - 1, False, 1, 0, 1)

            bodies(act, body, tail)

        @block.vector
        def _(dve):
            V = nc.vector
            dve.sem_inc(s_scan, 8)
            dve.sem_inc(s_rc, 2)
            dve.sem_inc(s_gated, RING)
            step = [0]

            def link(ins):
                step[0] += 1
                ins.then_inc(s_cst, 1)
                dve.wait_ge(s_cst, step[0])

            dve.wait_ge(s_ld, 16 * N_LOADS)
            link(V.memset(konst[:, 0:1], LN_EPS))
            link(V.tensor_copy(sel[:, :, :], hid[0:3 * GRP, 0, :].rearrange("p (r c) -> p r c", r=4)))
            link(V.tensor_copy(gsel[:, 0:4, :], hid[0:3 * E, 1, :].rearrange("p (r c) -> p r c", r=4)))
            link(V.tensor_copy(gsel[:, 4:6, :], hid[0:3 * E, 2, 0:2 * P].rearrange("p (r c) -> p r c", r=2)))
            link(V.tensor_copy(identb[:, :], ident[:, :]))
            link(V.tensor_scalar(w2[:, :, :], w2[:, :, :], scl[:, :], None, ALU.mult))
            link(V.tensor_scalar(b2f[:, :], b2f[:, :], scl[0:3 * E, :], None, ALU.mult))
            link(V.tensor_copy(b2s[:, 0, :], b2f[:, :]))
            link(V.tensor_tensor(b2r[:, :], b2f[:, :], b2s[:, 0, :], ALU.subtract))
            link(V.tensor_copy(b2s[:, 1, :], b2r[:, :]))
            link(V.tensor_tensor(b2s[:, 2, :], b2r[:, :], b2s[:, 1, :], ALU.subtract))
            link(V.tensor_scalar(w_g[0:C, :], w_in[:, :], gam[:, :], None, ALU.mult))
            link(V.tensor_scalar(wo0[:, :], wo0[:, :], 0.5, None, ALU.mult))
            link(V.tensor_scalar(wo1[:, :], wo1[:, :], 0.5, None, ALU.mult))
            for k in range(2):
                m = (P, DR)[k]
                if k == 0:
                    out, eye = diag[k][:, :], ident[:, :]
                else:
                    link(V.memset(diag[k][:, :], 0.0))
                    out = diag[k][:, :].rearrange("p (j c) -> p j c", j=4)[:, :, 0:QUART]
                    eye = ident[0:m, 0:m].rearrange("p (j c) -> p j c", j=4)
                link(V.tensor_scalar(out, eye, dvec[k][:, :], None, ALU.mult))
                for w, lo, c in ((w_d[k][:, DI:2 * P], RANK, CPT // 2), (w_c[k][:, :], RANK + NST, CPT)):
                    link(V.tensor_copy(w.rearrange("p (c s) -> p c s", c=c),
                                       wx[k][:, lo:lo + NST].unsqueeze(1).to_broadcast([m, c, NST])))
            dve.wait_ge(s_setup_act, 4)
            link(V.tensor_scalar(amat[:, :], amat[:, :], -1.0, None, ALU.mult))
            cw = ys0[0:C + 1, 0:TAPS * DI].rearrange("p (k c) -> p k c", k=TAPS)
            for k in range(TAPS):
                link(V.tensor_tensor(w_u[:, k, :], w_g[:, 0:DI], cw[:, k, :], ALU.mult))
            link(V.memset(ys0[0:C + 1, 1024:1024 + TAPS - 1], 0.0))
            link(V.memset(ys0[0:1, 2048:3072], 1.0))

            lg = dA[:, 2:4, :].rearrange("p a t -> p (a t)").rearrange("p (b e) -> p b e", e=E)
            with dve.Fori(0, IMGS) as i:
                for half in range(2):
                    dve.wait_ge(s_rt, i * 2 + half + 3)
                    V.tensor_tensor(lg[:, bass.ds(i * 32 + 16 * half, 16), :],
                                    ps[6 + half][:, 0:16 * E].rearrange("p (b e) -> p b e", e=E),
                                    rb[:, :].unsqueeze(1).to_broadcast([P, 16, E]), ALU.add).then_inc(s_rc, 1)
            dve.wait_ge(s_rc, 2 + 2 * IMGS)

            def tmp(a, b):
                return h[:, a:b, :].rearrange("p a t -> p (a t)").rearrange("p (b e) -> p b e", e=E)

            rank, cmp_, gate = tmp(0, 2), tmp(2, 4), tmp(4, 6)
            eg = dA[:, 0:2, :].rearrange("p a t -> p (a t)").rearrange("p (b e) -> p b e", e=E)
            mx = h[:, 6, 0:BLK]
            link(V.memset(rank, 0.0))
            for j in range(E):
                lj = lg[:, :, j:j + 1]
                if j > 0:
                    link(V.tensor_tensor(cmp_[:, :, 0:j], lj.to_broadcast([P, BLK, j]), lg[:, :, 0:j], ALU.is_gt))
                    link(V.tensor_tensor(rank[:, :, 0:j], rank[:, :, 0:j], cmp_[:, :, 0:j], ALU.add))
                if j < E - 1:
                    k = E - 1 - j
                    link(V.tensor_tensor(cmp_[:, :, j + 1:E], lj.to_broadcast([P, BLK, k]), lg[:, :, j + 1:E], ALU.is_ge))
                    link(V.tensor_tensor(rank[:, :, j + 1:E], rank[:, :, j + 1:E], cmp_[:, :, j + 1:E], ALU.add))
            link(V.tensor_scalar(rank, rank, 1.5, None, ALU.is_lt))
            link(V.reduce_max(mx, lg, AX.X))
            V.tensor_tensor(eg, lg, mx.unsqueeze(2).to_broadcast([P, BLK, E]), ALU.subtract).then_inc(s_gm, 1)
            dve.wait_ge(s_ge, 1)
            link(V.tensor_tensor(gate, eg, rank, ALU.mult))
            link(V.reduce_sum(mx, gate, AX.X))
            link(V.reciprocal(mx, mx))
            link(V.tensor_tensor(gate, gate, mx.unsqueeze(2).to_broadcast([P, BLK, E]), ALU.mult))
            link(V.tensor_copy(g3[:, :, 0:E], gate))
            link(V.tensor_tensor(gate, gate, g3[:, :, 0:E], ALU.subtract))
            link(V.tensor_copy(g3[:, :, E:2 * E], gate))
            link(V.tensor_tensor(g3[:, :, 2 * E:3 * E], gate, g3[:, :, E:2 * E], ALU.subtract))
            dve.sem_inc(s_ready, 1)

            def begin(u, name):
                bank, at = u.at[name]
                dve.wait_ge(s_pr[bank], at + 1)
                return p_w[bank]

            def free(u, name, ins):
                ins.then_inc(s_pf[u.at[name][0]], 1)

            def gate_hidden(m, pc, bank):
                dve.wait_ge(s_gr, pc * HT + (m + 1))
                dve.wait_ge(s_gelu, pc * HT + (m + 1))
                V.tensor_tensor(hid[:, m, :], p_ring[bank][:, :], hid[:, m, :], ALU.mult).then_inc(s_gated, 1)

            def residual(u, pc):
                out = begin(u, "Y2")
                dve.wait_ge(s_xp, pc * 16 + 16)
                dve.wait_ge(s_x2s, pc * 16 + 16)
                free(u, "Y2", V.tensor_tensor(x2p[:, :], out[0:C, :], xp[:, :], ALU.add))

            def centre(u):
                out = begin(u, "MU")
                dve.wait_ge(s_pf[1], u.at["Y2"][1] + 2)
                free(u, "MU", V.scalar_tensor_tensor(xc[:, :], out[0:C, :], -1.0, x2p[:, :], op0=ALU.mult, op1=ALU.add))

            def dt_sum(k, b):
                dve.wait_ge(s_sp[k], b * 3 + 3)
                v, r = ((S[:, 0, :], S[:, 1, :]), (S[0:DR, 2, :], rl1[:, :]))[k]
                V.tensor_tensor(v, v, r, ALU.add).then_inc(s_dts[k], 1)

            def dt_x(k, b, par):
                dve.wait_ge(s_dts[k], b + 1)
                out, v = ((S[:, 1, :], S[:, 0, :]), (S[DR:P, 2, :], S[0:DR, 2, :]))[k]
                V.tensor_tensor(out, v, xr[k][:, par, :], ALU.mult).then_inc(s_s, 1)

            def times_b(n, i, odd):
                if i == 0:
                    dve.wait_ge(s_b, n * 16 + 16)
                dve.wait_ge(s_dtx, n * NT + (i + 1))
                bank = p_ring[ring(odd).index(("tile", i)) % RING]
                V.tensor_tensor(bank[:, :], bank[:, :], bB[:, odd, :], ALU.mult).then_inc(s_mul, 1)

            def scan(n, i, rev, odd):
                if i % BATCH == 0:
                    dve.wait_ge(s_carry, n * NB + (i // BATCH + 5))
                dve.wait_ge(s_exp, n * NT + (i + 1 + 2))
                dve.wait_ge(s_hc, n * NT + (i - NH + 1 + 8))
                dve.wait_ge(s_mul, n * NT + (i + 1))
                bank = p_ring[ring(odd).index(("tile", i)) % RING]
                a, b, o = dA[:, i % NA, :], bank[:, :], h[:, i % NH, :]
                if rev:
                    a, b, o = a[:, ::-1], b[:, ::-1], o[:, ::-1]
                V.tensor_tensor_scan(o, a, b, carry[:, i:i + 1], ALU.mult, ALU.add).then_inc(s_scan, 1)

            def add_residual(u, f):
                out = begin(u, "OUT")
                dve.wait_ge(s_xf, f * 16 + 16)
                free(u, "OUT", V.tensor_tensor(xf[:, :], out[0:C, :], xf[:, :], ALU.add))

            with dve.Fori(0, NCH) as j:
                u = piece_uses(j)
                for m in range(HT):
                    gate_hidden(m, j, m % RING)
                residual(u, j)
                centre(u)
            for k in range(2):
                dt_sum(k, 0)
            for k in range(2):
                dt_x(k, 0, 0)
            times_b(0, 0, 0)

            def body(img, q, rev, odd, last, before, u):
                fin = before == 1
                n, pc = body_number(img, q, rev, odd), piece_number(img, q, rev)
                nxt = 1 - odd
                for i in range(NT):
                    if i == 6:
                        dt_sum(0, n + 1)
                    if i == 7:
                        dt_sum(1, n + 1)
                        dt_x(0, n + 1, nxt)
                    if i == 8:
                        dt_x(1, n + 1, nxt)
                    if i == 13 and fin:
                        add_residual(u, img * NCH + q * 2 + odd - 1)
                    if odd:
                        if i == 11:
                            residual(u, pc)
                        if i == 13:
                            centre(u)
                    for slot, m in GATES[odd]:
                        if slot == i:
                            gate_hidden(m, pc, ring(odd).index(("gate", m)) % RING)
                    if i + 1 < NT:
                        times_b(n, i + 1, odd)
                    else:
                        times_b(n + 1, 0, nxt)
                    scan(n, i, rev, odd)

            def tail(img, u):
                add_residual(u, img * NCH + (NCH - 1))

            bodies(dve, body, tail)

        @block.gpsimd
        def _(pool):
            G = nc.gpsimd
            pool.sem_inc(s_hc, 8)
            pool.sem_inc(s_r1, 1)
            pool.sem_inc(s_lo, 1)
            pool.sem_inc(s_xn, 1)
            pool.sem_inc(s_y, 2)
            pool.sem_inc(s_carry, NB - 1)
            G.memset(carry[:, :], 0.0).then_inc(s_carry, 1)

            def normalise(pc):
                pool.wait_ge(s_rs, pc + 1)
                pool.wait_ge(s_xns, pc * 16 + 16)
                G.tensor_tensor(xnp[:, :], xc[:, :], sq[:, :], ALU.mult).then_inc(s_xn, 1)

            def split_rest(b):
                pool.wait_ge(s_cast, b * 2 + 1)
                G.tensor_tensor(S[:, :, :], S[:, :, :], spl[:, 0, :, :], ALU.subtract).then_inc(s_r1, 1)

            def split_low(b):
                pool.wait_ge(s_cast, b * 2 + 2)
                G.tensor_tensor(spl[:, 2, :, :], S[:, :, :], spl[:, 1, :, :], ALU.subtract).then_inc(s_lo, 1)

            def gate_y(low, f, par, chunk, buf):
                y = yr1[:, buf, :] if low else yr0[:, :]
                G.tensor_tensor(y, y, (ys1 if low else ys0)[:, bass.ds(chunk * CH, CH)], ALU.add).then_inc(s_fin, 1)
                pool.wait_ge(s_fin, f * 4 + (3 if low else 1))
                G.tensor_tensor(y, y, (sz1 if low else sz0)[:, par, :], ALU.mult).then_inc(s_fin, 1)

            def times_c(n, i, par, reset):
                if i == 0:
                    pool.wait_ge(s_cast, n * 2 + 2)
                pool.wait_ge(s_scan, n * NT + (i + 1 + 8))
                if i % BATCH == 0:
                    pool.wait_ge(s_y, n * NB + (i // BATCH + 1))
                G.tensor_tensor(hc[:, i % NH, :], h[:, i % NH, :], cC[:, par, :], ALU.mult).then_inc(s_hc, 1)
                if i % BATCH == BATCH - 1:
                    cols = carry[:, i - BATCH + 1:i + 1]
                    if reset is None:
                        G.memset(cols, 0.0).then_inc(s_carry, 1)
                    else:
                        s0 = (i - BATCH + 1) % NH
                        G.tensor_copy(cols, h[:, s0:s0 + BATCH, reset]).then_inc(s_carry, 1)

            with pool.Fori(0, NCH) as j:
                normalise(j)
            split_rest(0)
            split_low(0)

            def body(img, q, rev, odd, last, before, u):
                fin = before == 1
                n, pc = body_number(img, q, rev, odd), piece_number(img, q, rev)
                par = odd
                reset = None if last and odd else (0 if rev else CH - 1)
                for i in range(NT):
                    if i in (5, 7) and fin:
                        pool.wait_ge(s_ready, 1)
                        pool.wait_ge(s_ev, n * 2 + 2)
                        gate_y(i == 7, img * NCH + q * 2 + odd - 1, odd, chunk_of(q, rev, odd) + 1, 1 - odd)
                    if i == 9:
                        split_rest(n + 1)
                    if i == 13:
                        split_low(n + 1)
                    if i == 17 and odd:
                        normalise(pc)
                    times_c(n, i, par, reset)

            def tail(img, u):
                pool.wait_ge(s_ready, 1)
                pool.wait_ge(s_ev, (img + 1) * (BODIES * 2) + 2)
                for low in (False, True):
                    gate_y(low, img * NCH + (NCH - 1), 0, 0, 1)

            bodies(pool, body, tail)


N_LOADS = 30


def low_layout(rows, end):
    low = np.zeros((P, rows.shape[1]), rows.dtype)
    for j in range(4):
        low[GRP * j:GRP * j + QUART] = rows[end - DR + QUART * j:end - DR + QUART * (j + 1)]
    return np.concatenate([rows[:end - DR], low])


def kernel(**inputs):
    import concourse.bacc as _bacc
    from concourse.bass_utils import run_bass_kernel_spmd as _run

    a = {k: np.asarray(v) for k, v in inputs.items()}
    L0, L1 = "L0_conv_", "L1_conv_"
    laid = {
        "x": a["x"].reshape(IMGS, C, PIX),
        "w1T": a[L0 + "fc1_w"].transpose(2, 0, 1).reshape(C, E * HID),
        "w2T": a[L0 + "fc2_w"].transpose(0, 2, 1).reshape(HT, P, C).transpose(1, 0, 2),
        "b1": a[L0 + "fc1_b"].reshape(HT, P).T,
        "b2": np.tile(a[L0 + "fc2_b"], (3, 1)),
        "wrT": a[L0 + "router_w"].T,
        "router_b": a[L0 + "router_b"],
        "scale": a[L0 + "scale"],
        "w_in": low_layout(a[L1 + "W_in"].T, 2 * DI).T,
        "gamma": a[L1 + "gamma"][:, None],
        "beta": a[L1 + "beta"][:, None],
        "conv_w": a[L1 + "conv_w"].T.reshape(-1),
        "conv_b": a[L1 + "conv_b"][:, None],
        "w_x": a[L1 + "W_xproj"],
        "w_xT": a[L1 + "W_xproj"][:, :RANK].T,
        "w_dt": a[L1 + "W_dt"],
        "b_dt": a[L1 + "b_dt"][:, None],
        "a_log": a[L1 + "A_log"].reshape(NT, P).T,
        "d": a[L1 + "D"][:, None],
        "w_out": a[L1 + "W_out"],
        "w_out_low": low_layout(a[L1 + "W_out"], DI)[P:2 * P],
    }
    laid.update(selectors())
    nc = _bacc.Bacc("TRN2", target_bir_lowering=False, num_devices=1)
    arrays, A = {}, {}
    for name, v in laid.items():
        v = np.ascontiguousarray(v)
        arrays[f"in_{name}"] = v
        A[name] = nc.dram_tensor(f"in_{name}", v.shape, mybir.dt.from_np(v.dtype), kind="ExternalInput").ap()
    A["out"] = nc.dram_tensor("out", [IMGS, C, PIX], mybir.dt.float32, kind="ExternalOutput").ap()
    moe_mamba(nc, A)
    r = _run(nc, [arrays], core_ids=[0])
    return r.results[0]["out"].reshape(IMGS, C, 64, 64)
```
